# Optimizing a Trainium2 kernel written in Bass

```python
import numpy as np
import jax
import jax.numpy as jnp

def _softmax(x, axis=-1):
    return jax.nn.softmax(x, axis=axis)

def _gelu(x):
    return jax.nn.gelu(x, approximate=True)

def _silu(x):
    return jax.nn.silu(x)

def _sigmoid(x):
    return jax.nn.sigmoid(x)

def _layernorm(x, axis=-1, eps=1e-05):
    m = jnp.mean(x, axis=axis, keepdims=True)
    v = jnp.var(x, axis=axis, keepdims=True)
    return (x - m) / jnp.sqrt(v + eps)

def _scatter_add(tgt, idx, src, axis=0):
    return tgt.at[idx].add(src)

def _segment_sum(src, seg, n):
    return jax.ops.segment_sum(src, seg, n)
kernel_name = 'mk_adaln_d1_jaxref_r8_0735a8'

def setup_inputs(seed: int=0):
    np.random.seed(seed)
    _w = jnp.asarray

    def _L0_attn_setup():
        import jax, jax.numpy as jnp
        import numpy as np
        B, T, D = (4, 512, 128)

        def _ssm(v, A, C):
            decay = jax.nn.sigmoid(A)
            vT = jnp.swapaxes(v, 0, 1)

            def step(h, vt):
                h = decay * h + vt
                return (h, h)
            h0 = jnp.zeros(vT.shape[1:], dtype=v.dtype)
            _, hs = jax.lax.scan(step, h0, vT)
            return jnp.swapaxes(hs, 0, 1) * C
        key = jax.random.key(seed)
        ks = jax.random.split(key, 7)
        s_in = 1.0 / np.sqrt(D)
        return {'x': jax.random.normal(ks[0], (B, T, D), dtype=jnp.float32), 'W_in': jax.random.uniform(ks[1], (D, 2 * D), jnp.float32, -s_in, s_in), 'b_in': jax.random.uniform(ks[2], (2 * D,), jnp.float32, -s_in, s_in), 'A': jax.random.normal(ks[3], (D,), dtype=jnp.float32), 'C': jax.random.normal(ks[4], (D,), dtype=jnp.float32), 'W_out': jax.random.uniform(ks[5], (D, D), jnp.float32, -s_in, s_in), 'b_out': jax.random.uniform(ks[6], (D,), jnp.float32, -s_in, s_in)}
    _L0_attn_in = _L0_attn_setup()

    def _L0_ffn_setup():
        import jax, jax.numpy as jnp
        import numpy as np
        THRESHOLD = 0.1
        key = jax.random.key(seed)
        k1, k2, k3 = jax.random.split(key, 3)
        B, S, D, E = (4, 512, 128, 8)
        inputs = jax.random.normal(k1, (B, S, D), dtype=jnp.float32)
        gate_w = jax.random.normal(k2, (D, E), dtype=jnp.float32) * 0.02
        gate_b = jnp.zeros((E,), dtype=jnp.float32)
        expert_w = jax.random.normal(k3, (E, D, D), dtype=jnp.float32) * 0.02
        expert_b = jnp.zeros((E, D), dtype=jnp.float32)
        return {'inputs': inputs, 'gate_w': gate_w, 'gate_b': gate_b, 'expert_w': expert_w, 'expert_b': expert_b}
    _L0_ffn_in = _L0_ffn_setup()
    _L0_c = _w((lambda *s: np.random.randn(*s).astype(np.float32) * 0.05)(8, 128))
    _L0_wmod = _w((lambda *s: np.random.randn(*s).astype(np.float32) * 0.05)(128, 6 * 128) * 128 ** (-0.5))
    _d = {'L0_attn_x': _L0_attn_in['x'], 'L0_attn_W_in': _L0_attn_in['W_in'], 'L0_attn_b_in': _L0_attn_in['b_in'], 'L0_attn_A': _L0_attn_in['A'], 'L0_attn_C': _L0_attn_in['C'], 'L0_attn_W_out': _L0_attn_in['W_out'], 'L0_attn_b_out': _L0_attn_in['b_out'], 'L0_ffn_gate_w': _L0_ffn_in['gate_w'], 'L0_ffn_gate_b': _L0_ffn_in['gate_b'], 'L0_ffn_expert_w': _L0_ffn_in['expert_w'], 'L0_ffn_expert_b': _L0_ffn_in['expert_b'], 'L0_c': _L0_c, 'L0_wmod': _L0_wmod}
    _x0 = _d['L0_attn_x']
    _d['L0_attn_x'] = jax.random.normal(jax.random.fold_in(jax.random.key(seed), 1), (8, 1024, 128), dtype=_x0.dtype)
    del _x0
    return _d

def reference(L0_attn_x, L0_attn_W_in, L0_attn_b_in, L0_attn_A, L0_attn_C, L0_attn_W_out, L0_attn_b_out, L0_ffn_gate_w, L0_ffn_gate_b, L0_ffn_expert_w, L0_ffn_expert_b, L0_c, L0_wmod):

    def _L0_attn_ref(x, W_in, b_in, A, C, W_out, b_out):
        import jax, jax.numpy as jnp
        import numpy as np
        B, T, D = (4, 512, 128)

        def _ssm(v, A, C):
            decay = jax.nn.sigmoid(A)
            vT = jnp.swapaxes(v, 0, 1)

            def step(h, vt):
                h = decay * h + vt
                return (h, h)
            h0 = jnp.zeros(vT.shape[1:], dtype=v.dtype)
            _, hs = jax.lax.scan(step, h0, vT)
            return jnp.swapaxes(hs, 0, 1) * C
        proj = x @ W_in + b_in
        v, gate = jnp.split(proj, 2, axis=-1)
        gate = jax.nn.sigmoid(gate)
        y = gate * _ssm(v, A, C)
        return y @ W_out + b_out

    def _L0_ffn_ref(inputs, gate_w, gate_b, expert_w, expert_b):
        import jax, jax.numpy as jnp
        import numpy as np
        THRESHOLD = 0.1
        d = inputs.shape[-1]
        x = inputs.reshape(-1, d)
        gate_logits = jax.nn.softmax(x @ gate_w + gate_b, axis=-1)
        selected = (gate_logits >= THRESHOLD).astype(x.dtype)
        weights = gate_logits * selected
        wsum = jnp.sum(weights, axis=-1, keepdims=True)
        weights = weights / jnp.where(wsum == 0, jnp.ones_like(wsum), wsum)
        E = expert_w.shape[0]
        out = jnp.zeros((x.shape[0], expert_w.shape[-1]), dtype=x.dtype)
        for e in range(E):
            out = out + weights[:, e:e + 1] * (x @ expert_w[e] + expert_b[e])
        return out.reshape(*inputs.shape[:-1], out.shape[-1])
    x = L0_attn_x
    mod = (_silu(L0_c) @ L0_wmod).reshape(L0_c.shape[0], 6, 1, -1)
    sa, ca, ga, sb, cb, gb = (mod[:, 0], mod[:, 1], mod[:, 2], mod[:, 3], mod[:, 4], mod[:, 5])
    ga = (2 * (ga >= 0) - 1) * jnp.maximum(jnp.abs(ga), 0.25)
    gb = (2 * (gb >= 0) - 1) * jnp.maximum(jnp.abs(gb), 0.25)
    h = _layernorm(x, axis=-1) * (1 + ca) + sa
    x = x + ga * _L0_attn_ref(h, L0_attn_W_in, L0_attn_b_in, L0_attn_A, L0_attn_C, L0_attn_W_out, L0_attn_b_out)
    h = _layernorm(x, axis=-1) * (1 + cb) + sb
    x = x + gb * _L0_ffn_ref(h, L0_ffn_gate_w, L0_ffn_gate_b, L0_ffn_expert_w, L0_ffn_expert_b)
    return x

_drawn_inputs = setup_inputs


def setup_inputs(seed=0):
    import zlib

    import numpy as np

    out = dict(_drawn_inputs(seed))
    spreads = {'L0_ffn_gate_b': (0.0, 0.8), 'L0_ffn_expert_b': (0.0, 0.777)}
    factors = {'L0_attn_b_in': 3.692, 'L0_attn_b_out': 4.289, 'L0_ffn_gate_w': 4.616}
    for name, (base, spread) in spreads.items():
        noise = np.random.default_rng([zlib.crc32(name.encode()), seed]).standard_normal(out[name].shape)
        drawn = base * np.exp(spread * noise) if base else spread * noise
        out[name] = jnp.asarray(drawn.astype(out[name].dtype))
    for name, factor in factors.items():
        out[name] = (out[name] * factor).astype(out[name].dtype)
    return out
```

```python
from contextlib import ExitStack

import concourse.bass as bass
from concourse import mybir

F32 = mybir.dt.float32
F32R = mybir.dt.float32r
BF16 = mybir.dt.bfloat16
I32 = mybir.dt.int32
ALU = mybir.AluOpType
ACT = mybir.ActivationFunctionType
AX = mybir.AxisListType

P = 128
TILES = 4
GROUP = TILES * P
LN_EPS = 1e-5
THRESHOLD = 0.1
GATE_FLOOR = 0.25
RSQRT_SEED = float(0x5F3759DF)
SLOTS = 4
RING = 4
HALVES = 8
DVE_HALF = 7
PART = 32


def adaln_kernel(nc, x_d, w_in_d, b_in_d, a_d, c_skip_d, w_out_d, b_out_d, gate_w_d, gate_b_d,
                 expert_w_d, expert_b_d, cond_d, wmod_d, out_d):
    batches, seq, d = x_d.shape
    experts = gate_w_d.shape[1]
    groups = batches * seq // GROUP
    per_batch = seq // GROUP
    assert d == P and experts == 8 and per_batch == 2 and groups % SLOTS == 0
    TE = TILES * experts
    first_looped, looped = 1, groups - SLOTS

    x_g = x_d.rearrange("b t d -> (b t) d").rearrange("(g j p) d -> g p j d", j=TILES, p=P)
    out_g = out_d.rearrange("b t d -> (b t) d").rearrange("(g j p) d -> g p j d", j=TILES, p=P)

    with ExitStack() as ctx:
        def sb(name, shape, dt=F32):
            return ctx.enter_context(nc.sbuf_tensor(name, shape, dt))

        def bank(name):
            return ctx.enter_context(nc.psum_tensor(name, [P, 512], F32))

        def sem(name):
            return ctx.enter_context(nc.semaphore(name))

        ident = sb("ident", [P, P])
        w_in = sb("w_in", [P, 2 * P])
        wmod = sb("wmod", [P, 6 * P])
        w_out = sb("w_out", [P, P])
        w_outc = sb("w_outc", [P, P])
        w_outg = sb("w_outg", [P, batches, P])
        gate_w = sb("gate_w", [P, experts])
        gate_b = sb("gate_b", [P, experts])
        expert_w = sb("expert_w", [P, experts * P])
        expert_w_hi = sb("expert_w_hi", [P, experts * P], F32R)
        expert_w_lo = sb("expert_w_lo", [P, experts * P], F32R)
        expert_b = sb("expert_b", [3 * TE, TILES * P])
        expert_b_parts = sb("expert_b_parts", [3 * TE, TILES * P], F32R)
        cond = sb("cond", [batches, P])
        cond_tanh = sb("cond_tanh", [batches, P])
        cond_silu2 = sb("cond_silu2", [batches, P])
        silu_t = sb("silu_t", [P, batches])
        mod_cols = sb("mod_cols", [P, 4, batches])
        a_col = sb("a_col", [P, 1])
        c_col = sb("c_col", [P, 1])
        c_half = sb("c_half", [P, 1])
        b_gate = sb("b_gate", [P, 1])
        b_gate_half = sb("b_gate_half", [P, 1])
        decay = sb("decay", [P, 1])
        a_tanh = sb("a_tanh", [P, 1])
        b_v_row = sb("b_v_row", [1, P])
        b_out_row = sb("b_out_row", [batches, P])
        res_row = sb("res_row", [1, P])
        res_rows = sb("res_rows", [batches, P])
        res_row_mid = sb("res_row_mid", [1, P])
        res_rows_mid = sb("res_rows_mid", [batches, P])
        b_v_parts = sb("b_v_parts", [3 * PART, P], BF16)
        ones_bf = sb("ones_bf", [3 * PART, GROUP], BF16)
        gab_parts = sb("gab_parts", [3 * PART, P], BF16)
        pick_bf = sb("pick_bf", [3 * PART, batches, P], BF16)
        pick = sb("pick", [batches, batches, P])
        g_abs = sb("g_abs", [batches, 2 * P])
        g_sign = sb("g_sign", [batches, 2 * P])
        g_rows = sb("g_rows", [batches, 2 * P])
        gb_all = sb("gb_all", [P, batches, P])

        x_in = sb("x_in", [P, SLOTS, GROUP])
        x1 = sb("x1", [P, SLOTS, GROUP])
        xn1 = sb("xn1", [P, 2, GROUP])
        xn2 = sb("xn2", [P, 2, GROUP])
        h1_t = sb("h1_t", [P, 2, GROUP])
        h2_t = sb("h2_t", [P, 2, GROUP])
        h2_hi = sb("h2_hi", [P, 2, GROUP], F32R)
        h2_lo = sb("h2_lo", [P, 2, GROUP], F32R)
        hs = sb("hs", [P, 2, GROUP])
        gate_th = sb("gate_th", [P, 2, GROUP])
        y_t = sb("y_t", [P, 2, GROUP])
        bn1 = sb("bn1", [P, TILES, 6])
        bn2 = sb("bn2", [P, TILES, 6])
        mean_var = sb("mean_var", [P, 2 * TILES, 2])
        var_e = sb("var_e", [P, 2 * TILES])
        half_bits = sb("half_bits", [P, 2 * TILES], I32)
        guess = sb("guess", [P, 2 * TILES])
        guess_t = sb("guess_t", [P, 2 * TILES])
        rstd = sb("rstd", [P, 2, 2 * TILES])
        neg_mean = sb("neg_mean", [P, 2, 2 * TILES])
        logit = sb("logit", [P, TILES, experts])
        l_max = sb("l_max", [P, TILES])
        l_sub = sb("l_sub", [P, TILES, experts])
        l_exp = sb("l_exp", [P, TILES, experts])
        l_sum = sb("l_sum", [P, TILES])
        keep = sb("keep", [P, TILES, experts])
        w_sum = sb("w_sum", [P, TILES])
        w_inv = sb("w_inv", [P, TILES])
        w_kept = sb("w_kept", [P, TILES, experts])
        wts = sb("wts", [P, 2, TILES, experts])
        w_parts = sb("w_parts", [P, 3, TE], F32R)
        w_parts_t = sb("w_parts_t", [3 * TE, 2, P], F32R)
        z = sb("z", [P, 2, TILES, experts, P])
        mix = sb("mix", [P, 2, TILES, P])
        mix_g = sb("mix_g", [P, 2, TILES, P])

        ring = [bank(f"ring{r}") for r in range(RING)]
        bank_a = bank("bank_a")
        bank_b = bank("bank_b")
        bank_v = bank("bank_v")
        bank_g = bank("bank_g")

        cond_in = sem("cond_in")
        early_in = sem("early_in")
        late_in = sem("late_in")
        bias_in = sem("bias_in")
        zeroed = sem("zeroed")
        ident_zero = sem("ident_zero")
        ident_ready = sem("ident_ready")
        lo_ready = sem("lo_ready")
        tanh_ready = sem("tanh_ready")
        silu_ready = sem("silu_ready")
        hi_ready = sem("hi_ready")
        gb_ready = sem("gb_ready")
        picks_ready = sem("picks_ready")
        silu2_ready = sem("silu2_ready")
        mod_ready = sem("mod_ready")
        guarded = sem("guarded")
        v_bias_ready = sem("v_bias_ready")
        outw_ready = sem("outw_ready")
        bias_parts_ready = sem("bias_parts_ready")
        prep_step = sem("prep_step")
        silu_t_done = sem("silu_t_done")
        mod_done = sem("mod_done")
        ga_done = sem("ga_done")
        gb_done = sem("gb_done")
        x_loaded = sem("x_loaded")
        x_ready = sem("x_ready")
        bn_done = sem("bn_done")
        stats_done = sem("stats_done")
        root_step = sem("root_step")
        rstd_ready = sem("rstd_ready")
        xn1_ready = sem("xn1_ready")
        xn2_ready = sem("xn2_ready")
        xt_ready = sem("xt_ready")
        h1_ready = sem("h1_ready")
        v_ready = sem("v_ready")
        g_ready = sem("g_ready")
        scan_done = sem("scan_done")
        gate_done = sem("gate_done")
        y_ready = sem("y_ready")
        o_ready = sem("o_ready")
        x1_ready = sem("x1_ready")
        x1t_ready = sem("x1t_ready")
        h2_ready = sem("h2_ready")
        h2_split = sem("h2_split")
        logit_ready = sem("logit_ready")
        logit_read = sem("logit_read")
        router_step = sem("router_step")
        sub_ready = sem("sub_ready")
        exp_ready = sem("exp_ready")
        w_ready = sem("w_ready")
        wp_ready = sem("wp_ready")
        wt_ready = sem("wt_ready")
        wt_copied = sem("wt_copied")
        bias_ready = sem("bias_ready")
        e_ready = [sem(f"e_ready{r}") for r in range(RING)]
        e_used = [sem(f"e_used{r}") for r in range(RING)]
        pair_added = sem("pair_added")
        chain_step = sem("chain_step")
        mix_step = sem("mix_step")
        mix_ready = sem("mix_ready")
        mixg_ready = sem("mixg_ready")
        out_ready = sem("out_ready")
        out_sent = sem("out_sent")
        x1_free = sem("x1_free")

        block = ctx.enter_context(nc.Block())

        def steps(eng, step, first, last):
            for s in range(first, first_looped):
                step(s, 0)
            with eng.Fori(0, looped // SLOTS) as i:
                for s in range(first_looped, first_looped + SLOTS):
                    step(s, i)
            for s in range(first_looped + looped, last + 1):
                step(s, 0)

        def wait_apart(eng, *waits):
            waits = [(semaphore, v if isinstance(v, int) else eng.to_reg(v)) for semaphore, v in waits]
            eng.wait_ge(ident_ready, 1)
            for semaphore, value in waits:
                eng.wait_ge(semaphore, value)

        def tile(buf, slot, j):
            return buf[:, slot, j * P:(j + 1) * P]

        def by_tile(ap):
            return ap.rearrange("p (j n) -> p j n", j=TILES)

        def slot_of(buf, g):
            if isinstance(g, int):
                return by_tile(buf[:, g % SLOTS, :])
            return buf[:, bass.ds(g % SLOTS, 1), :].rearrange("p s (j n) -> p (s j) n", j=TILES)

        @block.sync
        def _(sp):
            def arrived(g):
                sp.wait_ge(x_loaded, 16 * (g + 1))
                sp.sem_inc(x_ready, 1)

            def load(g):
                sp.dma_start(slot_of(x_in, g), x_g[g]).then_inc(x_loaded, 16)

            def refill(g):
                arrived(g + SLOTS - 1)
                wait_apart(sp, (x1_ready, g + 1))
                sp.dma_start(slot_of(x_in, g), x_g[g + SLOTS]).then_inc(x_loaded, 16)

            def store(g):
                wait_apart(sp, (out_ready, g + 1))
                sp.dma_start(out_g[g], slot_of(x1, g)).then_inc(out_sent, 16)
                sp.wait_ge(out_sent, 16 * (g + 1))
                sp.sem_inc(x1_free, 1)

            load(0)
            sp.sem_inc(x1_free, SLOTS)
            sp.dma_start(cond[:, :], cond_d).then_inc(cond_in, 16)
            sp.dma_start(wmod[:, :], wmod_d).then_inc(cond_in, 16)
            sp.dma_start(w_in[:, :], w_in_d).then_inc(early_in, 16)
            for g in range(1, SLOTS):
                arrived(g - 1)
                load(g)
            head = 3
            for g in range(head):
                refill(g)
            with sp.Fori(0, groups - SLOTS - head) as g:
                store(g)
                refill(g + head)
            arrived(groups - 1)
            sp.sem_inc(x_ready, 1)
            with sp.Fori(groups - SLOTS - head, groups) as g:
                store(g)
            sp.wait_ge(out_sent, 16 * groups)

        @block.gpsimd
        def _(pool):
            nc.gpsimd.memset(ident[:, :], 0.0).then_inc(ident_zero, 1)
            nc.gpsimd.memset(expert_b[:, :], 0.0).then_inc(zeroed, 1)
            pool.wait_ge(ident_zero, 1)
            nc.gpsimd.affine_select(out=ident[:, :], in_=ident[:, :], compare_op=ALU.not_equal,
                                    fill=1.0, base=0, pattern=[[-1, P]],
                                    channel_multiplier=1).then_inc(ident_ready, 1)
            nc.gpsimd.memset(b_v_parts[:, :], 0.0)
            nc.gpsimd.memset(gab_parts[:, :], 0.0)
            nc.gpsimd.memset(ones_bf[:, :], 1.0)
            nc.gpsimd.memset(pick_bf[:, :, :], 0.0).then_inc(zeroed, 1)

            def norm(src, slot_src, dst, pair, col):
                for j in range(TILES):
                    last = nc.gpsimd.tensor_scalar(
                        tile(dst, pair % 2, j), tile(src, slot_src, j),
                        neg_mean[:, pair % 2, col + j:col + j + 1],
                        rstd[:, pair % 2, col + j:col + j + 1], ALU.add, ALU.mult)
                return last

            def fold(g, t, q):
                for k in (2 * t, 2 * t + 1):
                    pool.wait_ge(e_used[k % RING], 2 * g + k // RING + 1 + 2 * q)
                nc.gpsimd.tensor_tensor(z[:, g % 2, t, 0:4, :], z[:, g % 2, t, 0:4, :],
                                        z[:, g % 2, t, 4:8, :], ALU.add).then_inc(pair_added, 1)

            def step(s, i):
                q = SLOTS * i
                g1, g0, gt = s + 1, s, s - 1
                E, T = 0 <= g0 < groups, 0 <= gt < groups
                if T:
                    fold(gt, 2, q)
                if g1 >= 2:
                    if g1 < groups:
                        wait_apart(pool, (rstd_ready, g1 + 3 + q), (x1t_ready, g1 - 1 + q))
                else:
                    pool.wait_ge(rstd_ready, g1 + 3)
                if 0 <= g1 < groups:
                    norm(x1, g1 % SLOTS, xn2, g1, 0).then_inc(xn2_ready, 1)
                if E:
                    fold(g0, 0, q)
                if T:
                    wait_apart(pool, (mix_ready, gt + 1 + q))
                    if gt == 0:
                        pool.wait_ge(gb_ready, 1)
                    b = gt // per_batch + (SLOTS // per_batch) * i
                    nc.gpsimd.tensor_tensor(
                        mix_g[:, gt % 2], mix[:, gt % 2],
                        gb_all[:, bass.ds(b, 1), :].to_broadcast([P, TILES, P]),
                        ALU.mult).then_inc(mixg_ready, 1)
                if 0 <= g1 + 2 < groups:
                    if g1 >= 0:
                        wait_apart(pool, (xt_ready, g1 + 1 + q))
                    norm(x_in, (g1 + 2) % SLOTS, xn1, g1, TILES).then_inc(xn1_ready, 1)
                if E:
                    fold(g0, 1, q)
                    pool.wait_ge(pair_added, 4 * g0 + 2 + 4 * q)
                    nc.gpsimd.tensor_tensor(z[:, g0 % 2, 0:2, 0:2, :], z[:, g0 % 2, 0:2, 0:2, :],
                                            z[:, g0 % 2, 0:2, 2:4, :], ALU.add).then_inc(pair_added, 1)
                if s == -3:
                    pool.wait_ge(hi_ready, 1)
                    nc.gpsimd.tensor_tensor(expert_w_lo[:, :], expert_w[:, :],
                                            expert_w_hi[:, :].bitcast(F32),
                                            ALU.subtract).then_inc(lo_ready, 1)

            steps(pool, step, -3, groups)

        @block.scalar
        def _(act):
            def column(v):
                return v.rearrange("(p o) -> p o", o=1)

            def row(v):
                return v.rearrange("(o n) -> o n", o=1)

            act.dma_start(a_col[:, :], column(a_d)).then_inc(early_in, 16)
            act.dma_start(b_gate[:, :], column(b_in_d[P:2 * P])).then_inc(early_in, 16)
            act.dma_start(c_col[:, :], column(c_skip_d)).then_inc(early_in, 16)
            act.dma_start(b_v_row[:, :], row(b_in_d[0:P])).then_inc(early_in, 16)
            act.dma_start(b_out_row[:, :], row(b_out_d).to_broadcast([batches, P])).then_inc(early_in, 16)
            act.dma_start(w_out[:, :], w_out_d).then_inc(late_in, 16)
            act.dma_start(gate_w[:, :], gate_w_d).then_inc(late_in, 16)
            act.dma_start(gate_b[:, :], row(gate_b_d).to_broadcast([P, experts])).then_inc(late_in, 16)
            for h in range(2):
                act.dma_start(
                    expert_w[:, h * 512:(h + 1) * 512].rearrange("p (e n) -> p e n", e=4),
                    expert_w_d[4 * h:4 * h + 4].rearrange("e d n -> d e n")).then_inc(late_in, 16)
            act.wait_ge(cond_in, 32)
            act.wait_ge(early_in, 16 * 6)
            nc.scalar.activation(cond_tanh[:, :], cond[:, :], ACT.Tanh, scale=0.5)
            nc.scalar.activation(a_tanh[:, :], a_col[:, :], ACT.Tanh, scale=0.5)
            nc.scalar.mul(b_gate_half[:, :], b_gate[:, :], 0.5)
            nc.scalar.mul(c_half[:, :], c_col[:, :], 0.5).then_inc(tanh_ready, 1)
            act.wait_ge(silu_t_done, 1)
            nc.scalar.mul(silu_t[:, :], bank_a[:, 0:batches], 0.5).then_inc(silu_ready, 1)
            act.wait_ge(zeroed, 1)
            for part in range(3):
                for t in range(TILES):
                    r = part * TE + t * experts
                    act.dma_start(expert_b[r:r + experts, t * P:(t + 1) * P], expert_b_d).then_inc(bias_in, 16)

            def late_prep():
                act.wait_ge(late_in, 16 * 5)
                nc.scalar.copy(expert_w_hi[:, :], expert_w[:, :]).then_inc(hi_ready, 1)
                act.wait_ge(bias_in, 16 * 3 * TILES)
                nc.scalar.copy(expert_b_parts[:, :], expert_b[:, :]).then_inc(hi_ready, 1)
                act.wait_ge(gb_done, 1)
                for h in range(2):
                    last = nc.scalar.copy(gb_all[:, 4 * h:4 * h + 4, :],
                                          ring[2 + h][:, :].rearrange("p (b n) -> p b n", b=4))
                last.then_inc(gb_ready, 1)

            def mod(k, b):
                return mod_cols[:, k, bass.ds(b, 1)]

            def weigh(g0, k, q):
                r, t, h = k % RING, k // 2, k % 2
                act.wait_ge(e_ready[r], 2 * g0 + k // RING + 1 + 2 * q)
                for e in range(4 * h, 4 * h + 4):
                    last = nc.scalar.activation(
                        z[:, g0 % 2, t, e, :], ring[r][:, (e % 4) * P:(e % 4 + 1) * P], ACT.Copy,
                        scale=wts[:, g0 % 2, t, e:e + 1])
                last.then_inc(e_used[r], 1)

            def step(s, i):
                q = SLOTS * i
                g2, g1, g0 = s + 2, s + 1, s
                bq = (SLOTS // per_batch) * i
                A, B, E = 0 <= g2 < groups, 0 <= g1 < groups, 0 <= g0 < groups
                if A:
                    if g2 == 0:
                        act.wait_ge(mod_ready, 1)
                    if g2 >= 2:
                        wait_apart(act, (xt_ready, g2 + 1 + q), (g_ready, g2 - 1 + q))
                    else:
                        act.wait_ge(xt_ready, g2 + 1)
                    b = g2 // per_batch + bq
                    nc.scalar.activation(h1_t[:, g2 % 2, :], bank_a[:, :], ACT.Identity,
                                         bias=mod(0, b), scale=mod(1, b)).then_inc(h1_ready, 1)
                if s == -2:
                    late_prep()
                if E:
                    act.wait_ge(wt_ready, g0 + 1 + q)
                    nc.scalar.copy(w_parts_t[:, g0 % 2, :], bank_g[0:3 * TE, 0:P]).then_inc(wt_copied, 1)
                    act.wait_ge(w_ready, g0 + 1 + q)
                    weigh(g0, 0, q)
                    weigh(g0, 1, q)
                if A:
                    act.wait_ge(g_ready, g2 + 1 + q)
                    if g2 >= 2:
                        act.wait_ge(y_ready, g2 - 1 + q)
                    nc.scalar.activation(gate_th[:, g2 % 2, :], bank_g[:, :], ACT.Tanh,
                                         bias=b_gate_half[:, 0:1], scale=0.5).then_inc(gate_done, 1)
                if E:
                    weigh(g0, 2, q)
                if B:
                    if g1 >= 2:
                        wait_apart(act, (x1t_ready, g1 + 1 + q), (h2_split, g1 - 1 + q),
                                   (e_ready[RING - 1], 2 * g1 - 2 + 2 * q))
                    else:
                        act.wait_ge(x1t_ready, g1 + 1)
                    b = g1 // per_batch + bq
                    nc.scalar.activation(h2_t[:, g1 % 2, :], bank_b[:, :], ACT.Identity,
                                         bias=mod(2, b), scale=mod(3, b))
                    nc.scalar.activation(h2_hi[:, g1 % 2, :], bank_b[:, :], ACT.Identity,
                                         bias=mod(2, b), scale=mod(3, b)).then_inc(h2_ready, 1)
                if E:
                    weigh(g0, 3, q)
                    weigh(g0, 4, q)
                if B:
                    act.wait_ge(sub_ready, g1 + 1 + q)
                    nc.scalar.activation(l_exp[:, :, :], l_sub[:, :, :], ACT.Exp).then_inc(exp_ready, 1)
                if E:
                    for k in range(5, DVE_HALF):
                        weigh(g0, k, q)

            steps(act, step, -2, groups - 1)

        @block.vector
        def _(dve):
            vec = nc.vector
            made = [0]

            def prep(ins):
                made[0] += 1
                ins.then_inc(prep_step, 1)
                dve.wait_ge(prep_step, made[0])

            def split_rows(src, rest, mid, dst, n):
                prep(vec.tensor_copy(dst[0:n, :], src))
                prep(vec.tensor_tensor(rest, src, dst[0:n, :], ALU.subtract))
                prep(vec.tensor_copy(dst[PART:PART + n, :], rest))
                prep(vec.tensor_copy(mid, dst[PART:PART + n, :]))
                prep(vec.tensor_tensor(rest, rest, mid, ALU.subtract))
                return vec.tensor_copy(dst[2 * PART:2 * PART + n, :], rest)

            def picks():
                one_hot = ident[0:batches, 0:batches].unsqueeze(2).to_broadcast([batches, batches, P])
                dve.wait_ge(ident_ready, 1)
                vec.tensor_copy(pick[:, :, :], one_hot)
                dve.wait_ge(zeroed, 2)
                for part in range(3):
                    last = vec.tensor_copy(pick_bf[PART * part:PART * part + batches, :, :], one_hot)
                last.then_inc(picks_ready, 1)

            def modulation():
                dve.wait_ge(mod_done, 1)
                for k, plus in ((0, 0.0), (1, 1.0), (2, 0.0), (3, 1.0)):
                    last = vec.tensor_scalar(mod_cols[:, k, :], bank_b[:, k * batches:(k + 1) * batches],
                                             plus, None, ALU.add)
                last.then_inc(mod_ready, 1)
                dve.wait_ge(mod_done, 2)
                rows = bank_v[0:batches, 0:2 * P]
                prep(vec.tensor_scalar(g_sign[:, :], rows, 0.0, 2.0, ALU.is_ge, ALU.mult))
                prep(vec.tensor_scalar(g_sign[:, :], g_sign[:, :], -1.0, None, ALU.add))
                prep(vec.tensor_tensor(g_abs[:, :], g_sign[:, :], rows, ALU.mult))
                vec.scalar_tensor_tensor(out=g_rows[:, :], in0=g_abs[:, :], scalar=GATE_FLOOR,
                                         in1=g_sign[:, :], op0=ALU.max, op1=ALU.mult).then_inc(guarded, 1)

            def v_bias():
                prep(vec.tensor_scalar(decay[:, :], a_tanh[:, :], 0.5, 0.5, ALU.mult, ALU.add))
                split_rows(b_v_row[:, :], res_row[:, :], res_row_mid[:, :], b_v_parts, 1) \
                    .then_inc(v_bias_ready, 1)

            def out_weights():
                dve.wait_ge(late_in, 16 * 5)
                prep(vec.tensor_scalar(w_outc[:, :], w_out[:, :], c_half[:, 0:1], None, ALU.mult))
                dve.wait_ge(ga_done, 1)
                for h in range(2):
                    vec.tensor_tensor(w_outg[:, 4 * h:4 * h + 4, :],
                                      ring[h][:, :].rearrange("p (b n) -> p b n", b=4),
                                      w_outc[:, :].unsqueeze(1).to_broadcast([P, 4, P]), ALU.mult)
                prep(vec.tensor_tensor(res_rows[:, :], g_rows[:, 0:P], b_out_row[:, :], ALU.mult))
                split_rows(res_rows[:, :], res_rows[:, :], res_rows_mid[:, :], gab_parts, batches) \
                    .then_inc(outw_ready, 1)

            def bias_parts():
                dve.wait_ge(hi_ready, 2)
                low = slice(2 * TE, 3 * TE)
                vec.tensor_tensor(expert_b_parts[low, :], expert_b[low, :],
                                  expert_b_parts[low, :].bitcast(F32), ALU.subtract) \
                    .then_inc(bias_parts_ready, 1)

            def stats(buf, g, bn, j):
                return vec.bn_stats(bn[:, j, :], tile(buf, g % SLOTS, j))

            ROOT = 11

            def root(n, pair, q):
                par = pair % 2
                if n:
                    dve.wait_ge(root_step, ROOT * (pair + 2) + n + ROOT * q)
                else:
                    dve.wait_ge(stats_done, pair + 3 + q)
                if n == 0:
                    vec.tensor_scalar(neg_mean[:, par, :], mean_var[:, :, 0], -1.0, None, ALU.mult)
                    ins = vec.tensor_scalar(var_e[:, :], mean_var[:, :, 1], LN_EPS, None, ALU.add)
                elif n == 1:
                    ins = vec.tensor_scalar(half_bits[:, :], var_e[:, :].bitcast(I32), 1, None,
                                            ALU.logical_shift_right)
                elif n == 2:
                    ins = vec.tensor_scalar(guess[:, :].bitcast(I32), half_bits[:, :], -1.0, RSQRT_SEED,
                                            ALU.mult, ALU.add)
                elif n % 3 == 0:
                    ins = vec.scalar_tensor_tensor(out=guess_t[:, :], in0=guess[:, :], scalar=-0.5,
                                                   in1=guess[:, :], op0=ALU.mult, op1=ALU.mult)
                elif n % 3 == 1:
                    ins = vec.tensor_tensor(guess_t[:, :], guess_t[:, :], var_e[:, :], ALU.mult)
                else:
                    dst = rstd[:, par, :] if n == ROOT else guess[:, :]
                    ins = vec.scalar_tensor_tensor(out=dst, in0=guess_t[:, :], scalar=1.5,
                                                   in1=guess[:, :], op0=ALU.add, op1=ALU.mult)
                ins.then_inc(rstd_ready if n == ROOT else root_step, 1)

            ROUTER = 7

            def router(n, g, q):
                def before(k):
                    dve.wait_ge(router_step, ROUTER * g + k + ROUTER * q)
                spread = [P, TILES, experts]
                if n == 0:
                    dve.wait_ge(logit_ready, g + 1 + q)
                    vec.tensor_tensor(logit[:, :, :],
                                      bank_v[:, 0:TE].rearrange("p (j e) -> p j e", j=TILES),
                                      gate_b[:, :].unsqueeze(1).to_broadcast(spread),
                                      ALU.add).then_inc(logit_read, 1)
                elif n == 1:
                    dve.wait_ge(logit_read, g + 1 + q)
                    vec.tensor_reduce(l_max[:, :], logit[:, :, :], AX.X, ALU.max).then_inc(router_step, 1)
                elif n == 2:
                    before(1)
                    vec.tensor_tensor(l_sub[:, :, :], logit[:, :, :],
                                      l_max[:, :].unsqueeze(2).to_broadcast(spread),
                                      ALU.subtract).then_inc(sub_ready, 1)
                elif n == 3:
                    dve.wait_ge(exp_ready, g + 1 + q)
                    vec.tensor_reduce(l_sum[:, :], l_exp[:, :, :], AX.X, ALU.add).then_inc(router_step, 1)
                elif n == 4:
                    before(2)
                    vec.scalar_tensor_tensor(out=keep[:, :, :], in0=l_sum[:, :].unsqueeze(2).to_broadcast(spread),
                                             scalar=THRESHOLD, in1=l_exp[:, :, :],
                                             op0=ALU.mult, op1=ALU.is_le).then_inc(router_step, 1)
                elif n == 5:
                    before(3)
                    vec.tensor_tensor(w_kept[:, :, :], keep[:, :, :], l_exp[:, :, :],
                                      ALU.mult).then_inc(router_step, 1)
                elif n == 6:
                    before(4)
                    vec.tensor_reduce(w_sum[:, :], w_kept[:, :, :], AX.X, ALU.add).then_inc(router_step, 1)
                elif n == 7:
                    before(5)
                    vec.reciprocal(w_inv[:, :], w_sum[:, :]).then_inc(router_step, 1)
                elif n == 8:
                    before(6)
                    if g >= 2:
                        dve.wait_ge(e_used[2], 2 * g - 2 + 2 * q)
                    vec.tensor_tensor(wts[:, g % 2], w_kept[:, :, :],
                                      w_inv[:, :].unsqueeze(2).to_broadcast(spread),
                                      ALU.mult).then_inc(w_ready, 1)
                elif n == 9:
                    dve.wait_ge(w_ready, g + 1 + q)
                    if g >= 1:
                        dve.wait_ge(wt_ready, g + q)
                    vec.tensor_copy(w_parts[:, 0:3:2, :],
                                    wts[:, g % 2].rearrange("p j e -> p (j e)").unsqueeze(1)
                                    .to_broadcast([P, 2, TE])).then_inc(router_step, 1)
                else:
                    before(7)
                    vec.tensor_tensor(w_parts[:, 1, :], wts[:, g % 2].rearrange("p j e -> p (j e)"),
                                      w_parts[:, 0, :].bitcast(F32), ALU.subtract).then_inc(wp_ready, 1)

            def chain(n, g, q):
                if n == 0:
                    dve.wait_ge(e_ready[3], 2 * g + 2 + 2 * q)
                    dve.wait_ge(e_used[2], 2 * g + 2 + 2 * q)
                else:
                    dve.wait_ge(chain_step, 3 * g + n + 3 * q)
                ins = vec.scalar_tensor_tensor(
                    out=z[:, g % 2, 3, 0, :], in0=ring[3][:, n * P:(n + 1) * P],
                    scalar=wts[:, g % 2, 3, 4 + n:5 + n], in1=z[:, g % 2, 3, 0, :],
                    op0=ALU.mult, op1=ALU.add)
                ins.then_inc(e_used[3] if n == 3 else chain_step, 1)

            def step(s, i):
                q = SLOTS * i
                g2, g1, gt = s + 2, s + 1, s - 1
                A, B, T = 0 <= g2 < groups, 0 <= g1 < groups, 0 <= gt < groups
                next_norm = 0 <= g2 + 2 < groups
                for n in range(ROOT + 1):
                    if B or 0 <= g1 + 2 < groups:
                        root(n, g1, q)
                    if T and 2 <= n < 6:
                        chain(n - 2, gt, q)
                    if T and n == 7:
                        dve.wait_ge(pair_added, 4 * gt + 3 + 4 * q)
                        vec.tensor_tensor(mix[:, gt % 2, 0:2, :], z[:, gt % 2, 0:2, 0, :],
                                          z[:, gt % 2, 0:2, 1, :], ALU.add)
                if T:
                    dve.wait_ge(pair_added, 4 * gt + 4 + 4 * q)
                    dve.wait_ge(e_used[3], 2 * gt + 2 + 2 * q)
                    vec.tensor_reduce(mix[:, gt % 2, 2:4, :],
                                      z[:, gt % 2, 2:4, 0:4, :].rearrange("p t e n -> p t n e"),
                                      AX.X, ALU.add).then_inc(mix_step, 1)
                    dve.wait_ge(bias_ready, gt + 1 + q)
                    dve.wait_ge(mix_step, gt + 1 + q)
                    vec.tensor_tensor(mix[:, gt % 2], mix[:, gt % 2], by_tile(bank_b[:, :]),
                                      ALU.add).then_inc(mix_ready, 1)
                if A:
                    if g2 == 0:
                        v_bias()
                    dve.wait_ge(v_ready, g2 + 1 + q)
                    if g2 % per_batch:
                        dve.wait_ge(scan_done, g2 + q)
                    vec.tensor_tensor_scan(
                        hs[:, g2 % 2, :], decay[:, 0:1].to_broadcast([P, GROUP]), bank_v[:, :],
                        hs[:, (g2 - 1) % 2, GROUP - 1:GROUP] if g2 % per_batch else 0.0,
                        ALU.mult, ALU.add).then_inc(scan_done, 1)
                    dve.wait_ge(scan_done, g2 + 1 + q)
                    dve.wait_ge(gate_done, g2 + 1 + q)
                    vec.scalar_tensor_tensor(out=y_t[:, g2 % 2, :], in0=gate_th[:, g2 % 2, :], scalar=1.0,
                                             in1=hs[:, g2 % 2, :], op0=ALU.add,
                                             op1=ALU.mult).then_inc(y_ready, 1)
                if g2 == 0:
                    out_weights()
                if g1 == 0:
                    bias_parts()
                if T:
                    dve.wait_ge(mixg_ready, gt + 1 + q)
                    vec.tensor_tensor(x1[:, gt % SLOTS, :],
                                      mix_g[:, gt % 2].rearrange("p j n -> p (j n)"),
                                      x1[:, gt % SLOTS, :], ALU.add).then_inc(out_ready, 1)
                if B:
                    dve.wait_ge(h2_ready, g1 + 1 + q)
                    vec.tensor_tensor(h2_lo[:, g1 % 2, :], h2_t[:, g1 % 2, :],
                                      h2_hi[:, g1 % 2, :].bitcast(F32),
                                      ALU.subtract).then_inc(h2_split, 1)
                if A:
                    dve.wait_ge(o_ready, g2 + 1 + q)
                    dve.wait_ge(x1_free, g2 + 1 + q)
                    vec.tensor_tensor(x1[:, g2 % SLOTS, :], bank_a[:, :], x_in[:, g2 % SLOTS, :],
                                      ALU.add).then_inc(x1_ready, 1)
                if next_norm:
                    dve.wait_ge(x_ready, g2 + 3 + q)
                todo = [(x_in, g2 + 2, bn1, j) for j in range(TILES) if next_norm]
                todo += [(x1, g2, bn2, j) for j in range(TILES) if A]
                for n in range(9):
                    if B:
                        router(n, g1, q)
                    for _ in range(3 if n == 2 else 1):
                        if todo:
                            if A and len(todo) == TILES:
                                dve.wait_ge(x1_ready, g2 + 1 + q)
                            last = stats(*todo.pop(0))
                if A or next_norm:
                    last.then_inc(bn_done, 1)
                if B:
                    router(9, g1, q)
                    router(10, g1, q)
                if A or next_norm:
                    wait_apart(dve, (bn_done, g2 + 3 + q))
                    for j in range(TILES):
                        if A:
                            last = vec.bn_aggr(mean_var[:, j, :], bn2[:, j, :])
                        if next_norm:
                            last = vec.bn_aggr(mean_var[:, TILES + j, :], bn1[:, j, :])
                    last.then_inc(stats_done, 1)

            vec.memset(mean_var[:, :, :], 1.0)
            picks()
            dve.wait_ge(tanh_ready, 1)
            vec.scalar_tensor_tensor(out=cond_silu2[:, :], in0=cond_tanh[:, :], scalar=1.0,
                                     in1=cond[:, :], op0=ALU.add, op1=ALU.mult).then_inc(silu2_ready, 1)
            step(-4, 0)
            modulation()
            steps(dve, step, -3, groups)

        @block.tensor
        def _(pe):
            mm = nc.tensor.matmul
            pe.wait_ge(ident_ready, 1)
            pe.wait_ge(silu2_ready, 1)
            nc.tensor.transpose(bank_a[:, 0:batches], cond_silu2[:, :],
                                ident[0:batches, 0:batches]).then_inc(silu_t_done, 1)
            pe.wait_ge(silu_ready, 1)
            pe.wait_ge(cond_in, 32)
            for k, section in enumerate((0, 1, 3, 4)):
                last = mm(bank_b[:, k * batches:(k + 1) * batches],
                          wmod[:, section * P:(section + 1) * P], silu_t[:, :], start=True, stop=True)
            last.then_inc(mod_done, 1)
            for k, section in enumerate((2, 5)):
                last = mm(bank_v[0:batches, k * P:(k + 1) * P], silu_t[:, :],
                          wmod[:, section * P:(section + 1) * P], start=True, stop=True)
            last.then_inc(mod_done, 1)

            def gate_rows():
                pe.wait_ge(picks_ready, 1)
                pe.wait_ge(guarded, 1)
                for k, done in ((0, ga_done), (1, gb_done)):
                    for b in range(batches):
                        last = mm(ring[2 * k + b // 4][:, (b % 4) * P:(b % 4 + 1) * P], pick[:, b, :],
                                  g_rows[:, k * P:(k + 1) * P], start=True, stop=True)
                    last.then_inc(done, 1)

            def turn(bank_x, src, par, done):
                for j in range(TILES):
                    last = nc.tensor.transpose(bank_x[:, j * P:(j + 1) * P], tile(src, par, j), ident[:, :])
                last.then_inc(done, 1)

            def half(k, g0, q):
                r, t, h = k % RING, k // 2, k % 2
                if g0 >= 1 or k >= RING:
                    pe.wait_ge(e_used[r], 2 * g0 + k // RING + 2 * q)
                cols = slice(4 * h * P, (4 * h + 4) * P)
                hi, lo = tile(h2_hi, g0 % 2, t), tile(h2_lo, g0 % 2, t)
                mm(ring[r][:, :], hi, expert_w_hi[:, cols], start=True, stop=False)
                mm(ring[r][:, :], hi, expert_w_lo[:, cols], start=False, stop=False)
                mm(ring[r][:, :], lo, expert_w_hi[:, cols], start=False, stop=True).then_inc(e_ready[r], 1)

            def step(s, i):
                q = SLOTS * i
                g2, g1, g0 = s + 2, s + 1, s
                bq = (SLOTS // per_batch) * i
                A, B, E = 0 <= g2 < groups, 0 <= g1 < groups, 0 <= g0 < groups
                if A:
                    pe.wait_ge(xn1_ready, g2 + 1 + q)
                    if g2 >= 1:
                        pe.wait_ge(x1_ready, g2 + q)
                    turn(bank_a, xn1, g2 % 2, xt_ready)
                if s == -2:
                    gate_rows()
                if s == 0:
                    pe.wait_ge(lo_ready, 1)
                    pe.wait_ge(outw_ready, 1)
                    pe.wait_ge(gb_ready, 1)
                if E:
                    pe.wait_ge(h2_split, g0 + 1 + q)
                    half(0, g0, q)
                    pe.wait_ge(wp_ready, g0 + 1 + q)
                    pe.wait_ge(gate_done, min(g2, groups) + q)
                    nc.tensor.transpose(bank_g[0:3 * TE, 0:P],
                                        w_parts[:, :, :].bitcast(F32).rearrange("p a b -> p (a b)"),
                                        ident[:, :]).then_inc(wt_ready, 1)
                    half(1, g0, q)
                if A:
                    pe.wait_ge(h1_ready, g2 + 1 + q)
                    if g2 == 0:
                        pe.wait_ge(early_in, 16 * 6)
                        pe.wait_ge(v_bias_ready, 1)
                    if g0 >= 0:
                        pe.wait_ge(logit_read, g0 + 1 + q)
                    mm(bank_v[:, :], b_v_parts[:, :], ones_bf[:, :], start=True, stop=False)
                    mm(bank_v[:, :], w_in[:, 0:P], h1_t[:, g2 % 2, :], start=False,
                       stop=True).then_inc(v_ready, 1)
                    if g0 >= 0:
                        pe.wait_ge(wt_copied, g0 + 1 + q)
                    mm(bank_g[:, :], w_in[:, P:2 * P], h1_t[:, g2 % 2, :], start=True,
                       stop=True).then_inc(g_ready, 1)
                if E:
                    half(2, g0, q)
                    half(3, g0, q)
                if B:
                    pe.wait_ge(xn2_ready, g1 + 1 + q)
                    if g0 >= 1:
                        pe.wait_ge(mix_ready, g0 + q)
                    turn(bank_b, xn2, g1 % 2, x1t_ready)
                if A:
                    pe.wait_ge(y_ready, g2 + 1 + q)
                    if g2 == 0:
                        pe.wait_ge(outw_ready, 1)
                    b = g2 // per_batch + bq
                    mm(bank_a[:, :], pick_bf[:, bass.ds(b, 1), :].rearrange("p b n -> p (b n)"),
                       gab_parts[:, :].unsqueeze(1).to_broadcast([3 * PART, TILES, P]),
                       start=True, stop=False)
                    for j in range(TILES):
                        last = mm(bank_a[:, j * P:(j + 1) * P], tile(y_t, g2 % 2, j),
                                  w_outg[:, bass.ds(b, 1), :].rearrange("p b n -> p (b n)"),
                                  start=False, stop=(j == TILES - 1))
                    last.then_inc(o_ready, 1)
                if E:
                    half(4, g0, q)
                if B:
                    pe.wait_ge(h2_ready, g1 + 1 + q)
                    if A:
                        pe.wait_ge(scan_done, g2 + 1 + q)
                    else:
                        pe.wait_ge(logit_read, g1)
                    for j in range(TILES):
                        last = mm(bank_v[:, j * experts:(j + 1) * experts], tile(h2_t, g1 % 2, j),
                                  gate_w[:, :], start=True, stop=True)
                    last.then_inc(logit_ready, 1)
                if E:
                    half(5, g0, q)
                    pe.wait_ge(wt_copied, g0 + 1 + q)
                    if s == 0:
                        pe.wait_ge(bias_parts_ready, 1)
                    if not B:
                        pe.wait_ge(mix_ready, g0)
                    mm(bank_b[:, :], w_parts_t[:, g0 % 2, :], expert_b_parts[:, :], start=True,
                       stop=True).then_inc(bias_ready, 1)
                    half(6, g0, q)
                    half(7, g0, q)

            steps(pe, step, -2, groups - 1)


_INS = ["L0_attn_x", "L0_attn_W_in", "L0_attn_b_in", "L0_attn_A", "L0_attn_C", "L0_attn_W_out",
        "L0_attn_b_out", "L0_ffn_gate_w", "L0_ffn_gate_b", "L0_ffn_expert_w", "L0_ffn_expert_b",
        "L0_c", "L0_wmod"]
_OUTS = [((8, 1024, 128), "float32")]


def kernel(**inputs):
    import numpy as _np
    import concourse.bacc as _bacc
    from concourse import mybir as _mybir
    from concourse.bass_utils import run_bass_kernel_spmd as _run

    nc = _bacc.Bacc("TRN2", target_bir_lowering=False, num_devices=1)
    arrays, args = {}, []
    for name in _INS:
        a = _np.ascontiguousarray(inputs[name])
        arrays[f"in_{name}_dram"] = a
        args.append(nc.dram_tensor(f"in_{name}_dram", a.shape, _mybir.dt.from_np(a.dtype), kind="ExternalInput").ap())
    for i, (shape, dtype) in enumerate(_OUTS):
        dt = _mybir.dt.from_np(_np.dtype(dtype))
        args.append(nc.dram_tensor(f"out_{i}_dram", shape, dt, kind="ExternalOutput").ap())
    adaln_kernel(nc, *args)
    r = _run(nc, [arrays], core_ids=[0])
    return r.results[0]["out_0_dram"]
```

```python
from contextlib import ExitStack

import concourse.bass as bass
from concourse import mybir

I32 = mybir.dt.int32
F32 = mybir.dt.float32
F32R = mybir.dt.float32r
BF16 = mybir.dt.bfloat16
ALU = mybir.AluOpType
ACT = mybir.ActivationFunctionType
AX = mybir.AxisListType

P = 128
TILES = 4
GROUP = TILES * P
LN_EPS = 1e-5
THRESHOLD = 0.1
GATE_FLOOR = 0.25
RSQRT_SEED = float(0x5F1FFFF9)
RSQRT_C, RSQRT_D = 0.703952253, 2.38924456
LAST_SCALE = 0.375
SLOTS = 4
RING = 4
HALVES = 8
DVE_HALF = 7
PART = 32


def adaln_kernel(nc, x_d, w_in_d, b_in_d, a_d, c_skip_d, w_out_d, b_out_d, gate_w_d, gate_b_d,
                 expert_w_d, expert_b_d, cond_d, wmod_d, out_d):
    batches, seq, d = x_d.shape
    experts = gate_w_d.shape[1]
    groups = batches * seq // GROUP
    per_batch = seq // GROUP
    assert d == P and experts == 8 and per_batch == 2 and groups % SLOTS == 0
    TE = TILES * experts
    first_looped, looped = 1, groups - SLOTS

    x_g = x_d.rearrange("b t d -> (b t) d").rearrange("(g j p) d -> g p j d", j=TILES, p=P)
    out_g = out_d.rearrange("b t d -> (b t) d").rearrange("(g j p) d -> g p j d", j=TILES, p=P)

    with ExitStack() as ctx:
        def sb(name, shape, dt=F32):
            return ctx.enter_context(nc.sbuf_tensor(name, shape, dt))

        def bank(name):
            return ctx.enter_context(nc.psum_tensor(name, [P, 512], F32))

        def sem(name):
            return ctx.enter_context(nc.semaphore(name))

        ident = sb("ident", [P, P])
        w_in = sb("w_in", [P, 2 * P])
        wmod = sb("wmod", [P, 6 * P])
        w_out = sb("w_out", [P, P])
        w_outc = sb("w_outc", [P, P])
        w_outg = sb("w_outg", [P, batches, P])
        gate_w = sb("gate_w", [P, experts])
        gate_b = sb("gate_b", [1, TE])
        gate_b_rest = sb("gate_b_rest", [1, TE])
        gate_b_mid = sb("gate_b_mid", [1, TE])
        gate_b_parts = sb("gate_b_parts", [3 * PART, TE], BF16)
        expert_w = sb("expert_w", [P, experts * P])
        expert_w_hi = sb("expert_w_hi", [P, experts * P], F32R)
        expert_w_lo = sb("expert_w_lo", [P, experts * P], F32R)
        expert_b = sb("expert_b", [3 * TE, TILES * P])
        expert_b_parts = sb("expert_b_parts", [3 * TE, TILES * P], F32R)
        cond = sb("cond", [batches, P])
        cond_tanh = sb("cond_tanh", [batches, P])
        cond_silu2 = sb("cond_silu2", [batches, P])
        silu_t = sb("silu_t", [P, batches])
        mod_cols = sb("mod_cols", [P, 4, batches])
        a_col = sb("a_col", [P, 1])
        c_col = sb("c_col", [P, 1])
        c_half = sb("c_half", [P, 1])
        b_gate = sb("b_gate", [P, 1])
        b_gate_half = sb("b_gate_half", [P, 1])
        decay = sb("decay", [P, 1])
        a_tanh = sb("a_tanh", [P, 1])
        b_v_row = sb("b_v_row", [1, P])
        b_out_row = sb("b_out_row", [batches, P])
        res_row = sb("res_row", [1, P])
        res_rows = sb("res_rows", [batches, P])
        res_row_mid = sb("res_row_mid", [1, P])
        res_rows_mid = sb("res_rows_mid", [batches, P])
        b_v_parts = sb("b_v_parts", [3 * PART, P], BF16)
        ones_bf = sb("ones_bf", [3 * PART, GROUP], BF16)
        gab_parts = sb("gab_parts", [3 * PART, P], BF16)
        pick_bf = sb("pick_bf", [3 * PART, batches, P], BF16)
        pick = sb("pick", [batches, batches, P])
        g_abs = sb("g_abs", [batches, 2 * P])
        g_sign = sb("g_sign", [batches, 2 * P])
        g_rows = sb("g_rows", [batches, 2 * P])
        gb_all = sb("gb_all", [P, batches, P])

        x_in = sb("x_in", [P, SLOTS, GROUP])
        x1 = sb("x1", [P, SLOTS, GROUP])
        xn1 = sb("xn1", [P, 2, GROUP])
        xn2 = sb("xn2", [P, 2, GROUP])
        h1_t = sb("h1_t", [P, 2, GROUP])
        h2_t = sb("h2_t", [P, 2, GROUP])
        h2_hi = sb("h2_hi", [P, 2, GROUP], F32R)
        h2_lo = sb("h2_lo", [P, 2, GROUP], F32R)
        hs = sb("hs", [P, 2, GROUP])
        gate_th = sb("gate_th", [P, 2, GROUP])
        y_t = sb("y_t", [P, 2, GROUP])
        bn1 = sb("bn1", [P, TILES, 6])
        bn2 = sb("bn2", [P, TILES, 6])
        mean_var = sb("mean_var", [P, 2 * TILES, 2])
        var_e = sb("var_e", [P, 2 * TILES])
        neg_mean = sb("neg_mean", [P, 2, 2 * TILES])
        half_bits = sb("half_bits", [P, 2 * TILES], I32)
        guess = sb("guess", [P, 2 * TILES])
        guess_t = sb("guess_t", [P, 2 * TILES])
        rstd = sb("rstd", [P, 2, 2 * TILES])
        l_max = sb("l_max", [P, TILES])
        l_sub = sb("l_sub", [P, TILES, experts])
        l_exp = sb("l_exp", [P, TILES, experts])
        l_sum = sb("l_sum", [P, TILES])
        keep = sb("keep", [P, TILES, experts])
        w_sum = sb("w_sum", [P, TILES])
        w_inv = sb("w_inv", [P, TILES])
        w_kept = sb("w_kept", [P, TILES, experts])
        wts = sb("wts", [P, 2, TILES, experts])
        w_parts = sb("w_parts", [P, 3, TE], F32R)
        w_parts_t = sb("w_parts_t", [3 * TE, 2, P], F32R)
        z = sb("z", [P, 2, TILES, experts, P])
        mix = sb("mix", [P, 2, TILES, P])
        mix_g = sb("mix_g", [P, 2, TILES, P])

        ring = [bank(f"ring{r}") for r in range(RING)]
        bank_a = bank("bank_a")
        bank_b = bank("bank_b")
        bank_v = bank("bank_v")
        bank_g = bank("bank_g")

        cond_in = sem("cond_in")
        early_in = sem("early_in")
        late_in = sem("late_in")
        bias_in = sem("bias_in")
        zeroed = sem("zeroed")
        ident_zero = sem("ident_zero")
        ident_ready = sem("ident_ready")
        lo_ready = sem("lo_ready")
        tanh_ready = sem("tanh_ready")
        silu_ready = sem("silu_ready")
        hi_ready = sem("hi_ready")
        gb_ready = sem("gb_ready")
        picks_ready = sem("picks_ready")
        silu2_ready = sem("silu2_ready")
        mod_ready = sem("mod_ready")
        guarded = sem("guarded")
        v_bias_ready = sem("v_bias_ready")
        gate_b_ready = sem("gate_b_ready")
        outw_ready = sem("outw_ready")
        bias_parts_ready = sem("bias_parts_ready")
        prep_step = sem("prep_step")
        silu_t_done = sem("silu_t_done")
        mod_done = sem("mod_done")
        ga_done = sem("ga_done")
        gb_done = sem("gb_done")
        x_loaded = sem("x_loaded")
        x_ready = sem("x_ready")
        bn1_done = sem("bn1_done")
        bn2_done = sem("bn2_done")
        stats_done = sem("stats_done")
        root_step = sem("root_step")
        rstd_ready = sem("rstd_ready")
        xn1_ready = sem("xn1_ready")
        xn2_ready = sem("xn2_ready")
        xt_ready = sem("xt_ready")
        h1_ready = sem("h1_ready")
        v_ready = sem("v_ready")
        g_ready = sem("g_ready")
        scan_done = sem("scan_done")
        gate_done = sem("gate_done")
        y_ready = sem("y_ready")
        o_ready = sem("o_ready")
        x1_ready = sem("x1_ready")
        x1t_ready = sem("x1t_ready")
        h2_ready = sem("h2_ready")
        h2_split = sem("h2_split")
        logit_ready = sem("logit_ready")
        router_step = sem("router_step")
        sub_ready = sem("sub_ready")
        exp_ready = sem("exp_ready")
        w_ready = sem("w_ready")
        hi_part_ready = sem("hi_part_ready")
        wp_ready = sem("wp_ready")
        wt_ready = sem("wt_ready")
        wt_copied = sem("wt_copied")
        bias_ready = sem("bias_ready")
        e_ready = [sem(f"e_ready{r}") for r in range(RING)]
        e_used = [sem(f"e_used{r}") for r in range(RING)]
        pair_added = sem("pair_added")
        mix_step = sem("mix_step")
        mix_ready = sem("mix_ready")
        mixg_ready = sem("mixg_ready")
        out_ready = sem("out_ready")
        out_sent = sem("out_sent")
        x1_free = sem("x1_free")

        block = ctx.enter_context(nc.Block())

        def steps(eng, step, first, last):
            for s in range(first, first_looped):
                step(s, 0)
            with eng.Fori(0, looped // SLOTS) as i:
                for s in range(first_looped, first_looped + SLOTS):
                    step(s, i)
            for s in range(first_looped + looped, last + 1):
                step(s, 0)

        def wait_apart(eng, *waits):
            waits = [(semaphore, v if isinstance(v, int) else eng.to_reg(v)) for semaphore, v in waits]
            eng.wait_ge(ident_ready, 1)
            for semaphore, value in waits:
                eng.wait_ge(semaphore, value)

        def tile(buf, slot, j):
            return buf[:, slot, j * P:(j + 1) * P]

        def by_tile(ap):
            return ap.rearrange("p (j n) -> p j n", j=TILES)

        def slot_of(buf, g):
            if isinstance(g, int):
                return by_tile(buf[:, g % SLOTS, :])
            return buf[:, bass.ds(g % SLOTS, 1), :].rearrange("p s (j n) -> p (s j) n", j=TILES)

        @block.sync
        def _(sp):
            def arrived(g):
                sp.wait_ge(x_loaded, 16 * (g + 1))
                sp.sem_inc(x_ready, 1)

            def load(g):
                sp.dma_start(slot_of(x_in, g), x_g[g]).then_inc(x_loaded, 16)

            def refill(g):
                wait_apart(sp, (x1_ready, g + 1))
                sp.dma_start(slot_of(x_in, g), x_g[g + SLOTS]).then_inc(x_loaded, 16)
                arrived(g + SLOTS)

            def store(g):
                wait_apart(sp, (out_ready, g + 1))
                sp.dma_start(out_g[g], slot_of(x1, g)).then_inc(out_sent, 16)
                sp.wait_ge(out_sent, 16 * (g + 1))
                sp.sem_inc(x1_free, 1)

            load(0)
            sp.sem_inc(x1_free, SLOTS)
            sp.sem_inc(mix_ready, 1)
            sp.dma_start(cond[:, :], cond_d).then_inc(cond_in, 16)
            sp.dma_start(wmod[:, :], wmod_d).then_inc(cond_in, 16)
            sp.dma_start(w_in[:, :], w_in_d).then_inc(early_in, 16)
            for g in range(1, SLOTS):
                arrived(g - 1)
                load(g)
            arrived(SLOTS - 1)
            head = 3
            for g in range(head):
                refill(g)
            with sp.Fori(0, groups - SLOTS - head) as g:
                store(g)
                refill(g + head)
            sp.sem_inc(x_ready, 2)
            with sp.Fori(groups - SLOTS - head, groups) as g:
                store(g)
            sp.wait_ge(out_sent, 16 * groups)

        @block.gpsimd
        def _(pool):
            nc.gpsimd.memset(ident[:, :], 0.0).then_inc(ident_zero, 1)
            nc.gpsimd.memset(expert_b[:, :], 0.0).then_inc(zeroed, 1)
            pool.wait_ge(ident_zero, 1)
            nc.gpsimd.affine_select(out=ident[:, :], in_=ident[:, :], compare_op=ALU.not_equal,
                                    fill=1.0, base=0, pattern=[[-1, P]],
                                    channel_multiplier=1).then_inc(ident_ready, 1)
            nc.gpsimd.memset(b_v_parts[:, :], 0.0)
            nc.gpsimd.memset(gab_parts[:, :], 0.0)
            nc.gpsimd.memset(gate_b_parts[:, :], 0.0)
            nc.gpsimd.memset(ones_bf[:, :], 1.0)
            nc.gpsimd.memset(pick_bf[:, :, :], 0.0).then_inc(zeroed, 1)

            def norm(src, slot_src, dst, pair, col):
                for j in range(TILES):
                    last = nc.gpsimd.tensor_scalar(
                        tile(dst, pair % 2, j), tile(src, slot_src, j),
                        neg_mean[:, pair % 2, col + j:col + j + 1],
                        rstd[:, pair % 2, col + j:col + j + 1], ALU.add, ALU.mult)
                return last

            def fold(g, t, q):
                for k in (2 * t, 2 * t + 1):
                    pool.wait_ge(e_used[k % RING], 2 * g + k // RING + 1 + 2 * q)
                nc.gpsimd.tensor_tensor(z[:, g % 2, t, 0:4, :], z[:, g % 2, t, 0:4, :],
                                        z[:, g % 2, t, 4:8, :], ALU.add).then_inc(pair_added, 1)

            def step(s, i):
                q = SLOTS * i
                g1, g0, gt = s + 1, s, s - 1
                E, T = 0 <= g0 < groups, 0 <= gt < groups
                if g1 >= 2:
                    if g1 < groups:
                        wait_apart(pool, (rstd_ready, g1 + 3 + q), (x1t_ready, g1 - 1 + q))
                else:
                    pool.wait_ge(rstd_ready, g1 + 3)
                if 0 <= g1 < groups:
                    norm(x1, g1 % SLOTS, xn2, g1, 0).then_inc(xn2_ready, 1)
                if T:
                    fold(gt, 2, q)
                if 0 <= g1 + 2 < groups:
                    if g1 >= 0:
                        wait_apart(pool, (xt_ready, g1 + 1 + q))
                    norm(x_in, (g1 + 2) % SLOTS, xn1, g1, TILES).then_inc(xn1_ready, 1)
                if E:
                    fold(g0, 0, q)
                    fold(g0, 1, q)
                if T:
                    wait_apart(pool, (mix_ready, gt + 2 + q))
                    if gt == 0:
                        pool.wait_ge(gb_ready, 1)
                    b = gt // per_batch + (SLOTS // per_batch) * i
                    nc.gpsimd.tensor_tensor(
                        mix_g[:, gt % 2], mix[:, gt % 2],
                        gb_all[:, bass.ds(b, 1), :].to_broadcast([P, TILES, P]),
                        ALU.mult).then_inc(mixg_ready, 1)
                if E:
                    pool.wait_ge(pair_added, 4 * g0 + 2 + 4 * q)
                    nc.gpsimd.tensor_tensor(z[:, g0 % 2, 0:2, 0:2, :], z[:, g0 % 2, 0:2, 0:2, :],
                                            z[:, g0 % 2, 0:2, 2:4, :], ALU.add).then_inc(pair_added, 1)
                if s == -3:
                    pool.wait_ge(hi_ready, 1)
                    nc.gpsimd.tensor_tensor(expert_w_lo[:, :], expert_w[:, :],
                                            expert_w_hi[:, :].bitcast(F32),
                                            ALU.subtract).then_inc(lo_ready, 1)

            steps(pool, step, -3, groups)

        @block.scalar
        def _(act):
            def column(v):
                return v.rearrange("(p o) -> p o", o=1)

            def row(v):
                return v.rearrange("(o n) -> o n", o=1)

            act.dma_start(a_col[:, :], column(a_d)).then_inc(early_in, 16)
            act.dma_start(b_gate[:, :], column(b_in_d[P:2 * P])).then_inc(early_in, 16)
            act.dma_start(c_col[:, :], column(c_skip_d)).then_inc(early_in, 16)
            act.dma_start(b_v_row[:, :], row(b_in_d[0:P])).then_inc(early_in, 16)
            act.dma_start(b_out_row[:, :], row(b_out_d).to_broadcast([batches, P])).then_inc(early_in, 16)
            act.dma_start(w_out[:, :], w_out_d).then_inc(late_in, 16)
            act.dma_start(gate_w[:, :], gate_w_d).then_inc(late_in, 16)
            act.dma_start(gate_b[:, :].rearrange("o (j e) -> o j e", j=TILES),
                          row(gate_b_d).unsqueeze(1).to_broadcast([1, TILES, experts])).then_inc(late_in, 16)
            for h in range(2):
                act.dma_start(
                    expert_w[:, h * 512:(h + 1) * 512].rearrange("p (e n) -> p e n", e=4),
                    expert_w_d[4 * h:4 * h + 4].rearrange("e d n -> d e n")).then_inc(late_in, 16)
            act.wait_ge(cond_in, 32)
            act.wait_ge(early_in, 16 * 6)
            nc.scalar.activation(cond_tanh[:, :], cond[:, :], ACT.Tanh, scale=0.5)
            nc.scalar.activation(a_tanh[:, :], a_col[:, :], ACT.Tanh, scale=0.5)
            nc.scalar.mul(b_gate_half[:, :], b_gate[:, :], 0.5)
            nc.scalar.mul(c_half[:, :], c_col[:, :], 0.5).then_inc(tanh_ready, 1)
            act.wait_ge(silu_t_done, 1)
            nc.scalar.mul(silu_t[:, :], bank_a[:, 0:batches], 0.5).then_inc(silu_ready, 1)
            act.wait_ge(zeroed, 1)
            for part in range(3):
                for t in range(TILES):
                    r = part * TE + t * experts
                    act.dma_start(expert_b[r:r + experts, t * P:(t + 1) * P], expert_b_d).then_inc(bias_in, 16)

            def late_prep():
                act.wait_ge(late_in, 16 * 5)
                nc.scalar.copy(expert_w_hi[:, :], expert_w[:, :]).then_inc(hi_ready, 1)
                act.wait_ge(bias_in, 16 * 3 * TILES)
                nc.scalar.copy(expert_b_parts[:, :], expert_b[:, :]).then_inc(hi_ready, 1)
                act.wait_ge(gb_done, 1)
                for h in range(2):
                    last = nc.scalar.copy(gb_all[:, 4 * h:4 * h + 4, :],
                                          ring[2 + h][:, :].rearrange("p (b n) -> p b n", b=4))
                last.then_inc(gb_ready, 1)

            def mod(k, b):
                return mod_cols[:, k, bass.ds(b, 1)]

            def weigh(g0, k, q):
                r, t, h = k % RING, k // 2, k % 2
                act.wait_ge(e_ready[r], 2 * g0 + k // RING + 1 + 2 * q)
                for e in range(4 * h, 4 * h + 4):
                    last = nc.scalar.activation(
                        z[:, g0 % 2, t, e, :], ring[r][:, (e % 4) * P:(e % 4 + 1) * P], ACT.Copy,
                        scale=wts[:, g0 % 2, t, e:e + 1])
                last.then_inc(e_used[r], 1)

            def step(s, i):
                q = SLOTS * i
                g2, g1, g0, gt = s + 2, s + 1, s, s - 1
                bq = (SLOTS // per_batch) * i
                A, B, E, T = 0 <= g2 < groups, 0 <= g1 < groups, 0 <= g0 < groups, 0 <= gt < groups
                if s == -2:
                    late_prep()
                if T:
                    weigh(gt, 6, q)
                if A:
                    act.wait_ge(g_ready, g2 + 1 + q)
                    if g2 >= 2:
                        act.wait_ge(y_ready, g2 - 1 + q)
                    nc.scalar.activation(gate_th[:, g2 % 2, :], bank_g[:, :], ACT.Tanh,
                                         bias=b_gate_half[:, 0:1], scale=0.5).then_inc(gate_done, 1)
                if E:
                    act.wait_ge(w_ready, g0 + 1 + q)
                    weigh(g0, 0, q)
                if B:
                    if g1 >= 2:
                        wait_apart(act, (x1t_ready, g1 + 1 + q), (h2_split, g1 - 1 + q),
                                   (e_ready[RING - 1], 2 * g1 - 2 + 2 * q))
                    else:
                        act.wait_ge(x1t_ready, g1 + 1)
                    b = g1 // per_batch + bq
                    nc.scalar.activation(h2_t[:, g1 % 2, :], bank_b[:, :], ACT.Identity,
                                         bias=mod(2, b), scale=mod(3, b))
                    nc.scalar.activation(h2_hi[:, g1 % 2, :], bank_b[:, :], ACT.Identity,
                                         bias=mod(2, b), scale=mod(3, b)).then_inc(h2_ready, 1)
                if E:
                    weigh(g0, 1, q)
                    weigh(g0, 2, q)
                if E:
                    weigh(g0, 3, q)
                if 0 <= g2 + 1 < groups:
                    if g2 + 1 == 0:
                        act.wait_ge(mod_ready, 1)
                    if g2 >= 1:
                        wait_apart(act, (xt_ready, g2 + 2 + q), (g_ready, g2 + q))
                    else:
                        act.wait_ge(xt_ready, g2 + 2)
                    b = (g2 + 1) // per_batch + bq
                    nc.scalar.activation(h1_t[:, (g2 + 1) % 2, :], bank_a[:, :], ACT.Identity,
                                         bias=mod(0, b), scale=mod(1, b)).then_inc(h1_ready, 1)
                if E:
                    weigh(g0, 4, q)
                    weigh(g0, 5, q)
                if E:
                    act.wait_ge(wt_ready, g0 + 1 + q)
                    nc.scalar.copy(w_parts_t[:, g0 % 2, :], bank_g[0:3 * TE, 0:P]).then_inc(wt_copied, 1)
                if B:
                    act.wait_ge(sub_ready, g1 + 1 + q)
                    nc.scalar.activation(l_exp[:, :, :], l_sub[:, :, :], ACT.Exp).then_inc(exp_ready, 1)

            steps(act, step, -3, groups)

        @block.vector
        def _(dve):
            vec = nc.vector
            made = [0]

            def prep(ins):
                made[0] += 1
                ins.then_inc(prep_step, 1)
                dve.wait_ge(prep_step, made[0])

            def split_rows(src, rest, mid, dst, n):
                prep(vec.tensor_copy(dst[0:n, :], src))
                prep(vec.tensor_tensor(rest, src, dst[0:n, :], ALU.subtract))
                prep(vec.tensor_copy(dst[PART:PART + n, :], rest))
                prep(vec.tensor_copy(mid, dst[PART:PART + n, :]))
                prep(vec.tensor_tensor(rest, rest, mid, ALU.subtract))
                return vec.tensor_copy(dst[2 * PART:2 * PART + n, :], rest)

            def picks():
                one_hot = ident[0:batches, 0:batches].unsqueeze(2).to_broadcast([batches, batches, P])
                dve.wait_ge(ident_ready, 1)
                vec.tensor_copy(pick[:, :, :], one_hot)
                dve.wait_ge(zeroed, 2)
                for part in range(3):
                    last = vec.tensor_copy(pick_bf[PART * part:PART * part + batches, :, :], one_hot)
                last.then_inc(picks_ready, 1)

            def modulation():
                dve.wait_ge(mod_done, 1)
                for k, plus in ((0, 0.0), (1, 1.0), (2, 0.0), (3, 1.0)):
                    last = vec.tensor_scalar(mod_cols[:, k, :], bank_b[:, k * batches:(k + 1) * batches],
                                             plus, None, ALU.add)
                last.then_inc(mod_ready, 1)
                dve.wait_ge(mod_done, 2)
                rows = bank_v[0:batches, 0:2 * P]
                prep(vec.tensor_scalar(g_sign[:, :], rows, 0.0, 2.0, ALU.is_ge, ALU.mult))
                prep(vec.tensor_scalar(g_sign[:, :], g_sign[:, :], -1.0, None, ALU.add))
                prep(vec.tensor_tensor(g_abs[:, :], g_sign[:, :], rows, ALU.mult))
                vec.scalar_tensor_tensor(out=g_rows[:, :], in0=g_abs[:, :], scalar=GATE_FLOOR,
                                         in1=g_sign[:, :], op0=ALU.max, op1=ALU.mult).then_inc(guarded, 1)

            def v_bias():
                prep(vec.tensor_scalar(decay[:, :], a_tanh[:, :], 0.5, 0.5, ALU.mult, ALU.add))
                split_rows(b_v_row[:, :], res_row[:, :], res_row_mid[:, :], b_v_parts, 1) \
                    .then_inc(v_bias_ready, 1)

            def out_weights():
                dve.wait_ge(late_in, 16 * 5)
                split_rows(gate_b[:, :], gate_b_rest[:, :], gate_b_mid[:, :], gate_b_parts, 1) \
                    .then_inc(gate_b_ready, 1)
                prep(vec.tensor_scalar(w_outc[:, :], w_out[:, :], c_half[:, 0:1], None, ALU.mult))
                dve.wait_ge(ga_done, 1)
                for h in range(2):
                    vec.tensor_tensor(w_outg[:, 4 * h:4 * h + 4, :],
                                      ring[h][:, :].rearrange("p (b n) -> p b n", b=4),
                                      w_outc[:, :].unsqueeze(1).to_broadcast([P, 4, P]), ALU.mult)
                prep(vec.tensor_tensor(res_rows[:, :], g_rows[:, 0:P], b_out_row[:, :], ALU.mult))
                split_rows(res_rows[:, :], res_rows[:, :], res_rows_mid[:, :], gab_parts, batches) \
                    .then_inc(outw_ready, 1)

            def bias_parts():
                dve.wait_ge(hi_ready, 2)
                low = slice(2 * TE, 3 * TE)
                vec.tensor_tensor(expert_b_parts[low, :], expert_b[low, :],
                                  expert_b_parts[low, :].bitcast(F32), ALU.subtract) \
                    .then_inc(bias_parts_ready, 1)

            def stats(buf, g, bn, j):
                return vec.bn_stats(bn[:, j, :], tile(buf, g % SLOTS, j))

            ROOT = 9

            def root(n, pair, q):
                par = pair % 2
                if n:
                    dve.wait_ge(root_step, ROOT * (pair + 2) + n + ROOT * q)
                else:
                    dve.wait_ge(stats_done, pair + 3 + q)
                if n == 0:
                    vec.tensor_scalar(neg_mean[:, par, :], mean_var[:, :, 0], -1.0, None, ALU.mult)
                    ins = vec.tensor_scalar(var_e[:, :], mean_var[:, :, 1], LN_EPS, None, ALU.add)
                elif n == 1:
                    ins = vec.tensor_scalar(half_bits[:, :], var_e[:, :].bitcast(I32), 1, None,
                                            ALU.logical_shift_right)
                elif n == 2:
                    ins = vec.tensor_scalar(guess[:, :].bitcast(I32), half_bits[:, :], -1.0, RSQRT_SEED,
                                            ALU.mult, ALU.add)
                elif n == 3:
                    ins = vec.scalar_tensor_tensor(out=guess_t[:, :], in0=guess[:, :],
                                                   scalar=-LAST_SCALE * RSQRT_C, in1=guess[:, :],
                                                   op0=ALU.mult, op1=ALU.mult)
                elif n == 5:
                    ins = vec.scalar_tensor_tensor(out=guess[:, :], in0=guess_t[:, :],
                                                   scalar=LAST_SCALE * RSQRT_C * RSQRT_D, in1=guess[:, :],
                                                   op0=ALU.add, op1=ALU.mult)
                elif n == 6:
                    ins = vec.scalar_tensor_tensor(out=guess_t[:, :], in0=guess[:, :],
                                                   scalar=LAST_SCALE ** -2, in1=guess[:, :],
                                                   op0=ALU.mult, op1=ALU.mult)
                elif n in (4, 7):
                    ins = vec.tensor_tensor(guess_t[:, :], guess_t[:, :], var_e[:, :], ALU.mult)
                elif n == 8:
                    ins = vec.scalar_tensor_tensor(out=guess_t[:, :], in0=guess_t[:, :], scalar=-10.0 / 3.0,
                                                   in1=guess_t[:, :], op0=ALU.add, op1=ALU.mult)
                else:
                    ins = vec.scalar_tensor_tensor(out=rstd[:, par, :], in0=guess_t[:, :], scalar=5.0,
                                                   in1=guess[:, :], op0=ALU.add, op1=ALU.mult)
                ins.then_inc(rstd_ready if n == ROOT else root_step, 1)

            ROUTER, ROUTER_ALL = 6, 10

            def router(n, g, q):
                def before(k):
                    dve.wait_ge(router_step, ROUTER * g + k + ROUTER * q)
                spread = [P, TILES, experts]
                logit = bank_b[:, 0:TE].rearrange("p (j e) -> p j e", j=TILES)
                if n == 0:
                    dve.wait_ge(logit_ready, g + 1 + q)
                    vec.tensor_reduce(l_max[:, :], logit, AX.X, ALU.max).then_inc(router_step, 1)
                elif n == 1:
                    before(1)
                    vec.tensor_tensor(l_sub[:, :, :], logit,
                                      l_max[:, :].unsqueeze(2).to_broadcast(spread),
                                      ALU.subtract).then_inc(sub_ready, 1)
                elif n == 2:
                    dve.wait_ge(exp_ready, g + 1 + q)
                    vec.tensor_reduce(l_sum[:, :], l_exp[:, :, :], AX.X, ALU.add).then_inc(router_step, 1)
                elif n == 3:
                    before(2)
                    vec.scalar_tensor_tensor(out=keep[:, :, :], in0=l_sum[:, :].unsqueeze(2).to_broadcast(spread),
                                             scalar=THRESHOLD, in1=l_exp[:, :, :],
                                             op0=ALU.mult, op1=ALU.is_le).then_inc(router_step, 1)
                elif n == 4:
                    before(3)
                    vec.tensor_tensor(w_kept[:, :, :], keep[:, :, :], l_exp[:, :, :],
                                      ALU.mult).then_inc(router_step, 1)
                elif n == 5:
                    before(4)
                    vec.tensor_reduce(w_sum[:, :], w_kept[:, :, :], AX.X, ALU.add).then_inc(router_step, 1)
                elif n == 6:
                    before(5)
                    vec.reciprocal(w_inv[:, :], w_sum[:, :]).then_inc(router_step, 1)
                elif n == 7:
                    before(6)
                    if g >= 2:
                        dve.wait_ge(e_used[2], 2 * g - 2 + 2 * q)
                    vec.tensor_tensor(wts[:, g % 2], w_kept[:, :, :],
                                      w_inv[:, :].unsqueeze(2).to_broadcast(spread),
                                      ALU.mult).then_inc(w_ready, 1)
                elif n == 8:
                    dve.wait_ge(w_ready, g + 1 + q)
                    if g >= 1:
                        dve.wait_ge(wt_ready, g + q)
                    vec.tensor_copy(w_parts[:, 0:3:2, :],
                                    wts[:, g % 2].rearrange("p j e -> p (j e)").unsqueeze(1)
                                    .to_broadcast([P, 2, TE])).then_inc(hi_part_ready, 1)
                else:
                    dve.wait_ge(hi_part_ready, g + 1 + q)
                    vec.tensor_tensor(w_parts[:, 1, :], wts[:, g % 2].rearrange("p j e -> p (j e)"),
                                      w_parts[:, 0, :].bitcast(F32), ALU.subtract).then_inc(wp_ready, 1)

            def weigh_last(n, g, q):
                if n == 0:
                    dve.wait_ge(e_ready[3], 2 * g + 2 + 2 * q)
                    dve.wait_ge(e_used[2], 2 * g + 2 + 2 * q)
                ins = vec.scalar_tensor_tensor(
                    out=z[:, g % 2, 3, n, :], in0=ring[3][:, n * P:(n + 1) * P],
                    scalar=wts[:, g % 2, 3, 4 + n:5 + n], in1=z[:, g % 2, 3, n, :],
                    op0=ALU.mult, op1=ALU.add)
                if n == 3:
                    ins.then_inc(e_used[3], 1)

            def step(s, i):
                q = SLOTS * i
                g2, g1, g0, gt = s + 2, s + 1, s, s - 1
                A, B, E, T = 0 <= g2 < groups, 0 <= g1 < groups, 0 <= g0 < groups, 0 <= gt < groups
                next_norm = 0 <= g2 + 2 < groups
                more_x = 0 <= g2 + 3 < groups

                def x_stats(j):
                    if more_x:
                        if j == 0:
                            dve.wait_ge(x_ready, g2 + 4 + q)
                        ins = stats(x_in, g2 + 3, bn1, j)
                        if j == TILES - 1:
                            ins.then_inc(bn1_done, 1)

                if A:
                    dve.wait_ge(gate_done, g2 + 1 + q)
                    dve.wait_ge(scan_done, g2 + 1 + q)
                    vec.scalar_tensor_tensor(out=y_t[:, g2 % 2, :], in0=gate_th[:, g2 % 2, :], scalar=1.0,
                                             in1=hs[:, g2 % 2, :], op0=ALU.add,
                                             op1=ALU.mult).then_inc(y_ready, 1)
                if T:
                    dve.wait_ge(pair_added, 4 * gt + 3 + 4 * q)
                    vec.tensor_tensor(mix[:, gt % 2, 0:2, :], z[:, gt % 2, 0:2, 0, :],
                                      z[:, gt % 2, 0:2, 1, :], ALU.add)
                    dve.wait_ge(pair_added, 4 * gt + 4 + 4 * q)
                    dve.wait_ge(e_used[3], 2 * gt + 2 + 2 * q)
                    vec.tensor_reduce(mix[:, gt % 2, 2:4, :],
                                      z[:, gt % 2, 2:4, 0:4, :].rearrange("p t e n -> p t n e"),
                                      AX.X, ALU.add).then_inc(mix_step, 1)
                if g2 == 0:
                    out_weights()
                if g1 == 0:
                    bias_parts()
                if A:
                    dve.wait_ge(o_ready, g2 + 1 + q)
                    dve.wait_ge(x1_free, g2 + 1 + q)
                    vec.tensor_tensor(x1[:, g2 % SLOTS, :], bank_a[:, :], x_in[:, g2 % SLOTS, :],
                                      ALU.add).then_inc(x1_ready, 1)
                    dve.wait_ge(x1_ready, g2 + 1 + q)
                    for j in range(TILES):
                        last = stats(x1, g2, bn2, j)
                    last.then_inc(bn2_done, 1)
                if A or next_norm:
                    if A:
                        wait_apart(dve, (bn2_done, g2 + 1 + q))
                    else:
                        dve.wait_ge(bn1_done, g2 + 3)
                    for j in range(TILES):
                        if A:
                            last = vec.bn_aggr(mean_var[:, j, :], bn2[:, j, :])
                        if next_norm:
                            last = vec.bn_aggr(mean_var[:, TILES + j, :], bn1[:, j, :])
                    last.then_inc(stats_done, 1)
                for n in range(ROOT + 1):
                    if A or next_norm:
                        root(n, g2, q)
                    if n == 0:
                        x_stats(0)
                    if n == 1 and T:
                        dve.wait_ge(bias_ready, gt + 1 + q)
                        dve.wait_ge(mix_step, gt + 1 + q)
                        vec.tensor_tensor(mix[:, gt % 2], mix[:, gt % 2], by_tile(bank_v[:, :]),
                                          ALU.add).then_inc(mix_ready, 1)
                    if n == 3:
                        x_stats(1)
                    if n == 4 and B:
                        dve.wait_ge(h2_ready, g1 + 1 + q)
                        vec.tensor_tensor(h2_lo[:, g1 % 2, :], h2_t[:, g1 % 2, :],
                                          h2_hi[:, g1 % 2, :].bitcast(F32),
                                          ALU.subtract).then_inc(h2_split, 1)
                    if n == 5:
                        x_stats(2)
                    if n >= 6 and n < 8 and B:
                        router(n - 6, g1, q)
                    if n == 8:
                        x_stats(3)
                if 0 <= g2 + 1 < groups:
                    if g2 + 1 == 0:
                        v_bias()
                    dve.wait_ge(v_ready, g2 + 2 + q)
                    if (g2 + 1) % per_batch:
                        dve.wait_ge(scan_done, g2 + 1 + q)
                    vec.tensor_tensor_scan(
                        hs[:, (g2 + 1) % 2, :], decay[:, 0:1].to_broadcast([P, GROUP]), bank_v[:, :],
                        hs[:, g2 % 2, GROUP - 1:GROUP] if (g2 + 1) % per_batch else 0.0,
                        ALU.mult, ALU.add).then_inc(scan_done, 1)
                for n in range(2, ROUTER_ALL):
                    if B:
                        router(n, g1, q)
                    if E and 4 <= n < 8:
                        weigh_last(n - 4, g0, q)
                    if n == 3 and T:
                        dve.wait_ge(mixg_ready, gt + 1 + q)
                        vec.tensor_tensor(x1[:, gt % SLOTS, :],
                                          mix_g[:, gt % 2].rearrange("p j n -> p (j n)"),
                                          x1[:, gt % SLOTS, :], ALU.add).then_inc(out_ready, 1)

            vec.memset(mean_var[:, :, :], 1.0)
            picks()
            dve.wait_ge(tanh_ready, 1)
            vec.scalar_tensor_tensor(out=cond_silu2[:, :], in0=cond_tanh[:, :], scalar=1.0,
                                     in1=cond[:, :], op0=ALU.add, op1=ALU.mult).then_inc(silu2_ready, 1)
            step(-5, 0)
            step(-4, 0)
            modulation()
            steps(dve, step, -3, groups)

        @block.tensor
        def _(pe):
            mm = nc.tensor.matmul
            pe.wait_ge(ident_ready, 1)
            pe.wait_ge(silu2_ready, 1)
            nc.tensor.transpose(bank_a[:, 0:batches], cond_silu2[:, :],
                                ident[0:batches, 0:batches]).then_inc(silu_t_done, 1)
            pe.wait_ge(silu_ready, 1)
            pe.wait_ge(cond_in, 32)
            for k, section in enumerate((0, 1, 3, 4)):
                last = mm(bank_b[:, k * batches:(k + 1) * batches],
                          wmod[:, section * P:(section + 1) * P], silu_t[:, :], start=True, stop=True)
            last.then_inc(mod_done, 1)
            for k, section in enumerate((2, 5)):
                last = mm(bank_v[0:batches, k * P:(k + 1) * P], silu_t[:, :],
                          wmod[:, section * P:(section + 1) * P], start=True, stop=True)
            last.then_inc(mod_done, 1)

            def gate_rows():
                pe.wait_ge(picks_ready, 1)
                pe.wait_ge(guarded, 1)
                for k, done in ((0, ga_done), (1, gb_done)):
                    for b in range(batches):
                        last = mm(ring[2 * k + b // 4][:, (b % 4) * P:(b % 4 + 1) * P], pick[:, b, :],
                                  g_rows[:, k * P:(k + 1) * P], start=True, stop=True)
                    last.then_inc(done, 1)

            def turn(bank_x, src, par, done):
                for j in range(TILES):
                    last = nc.tensor.transpose(bank_x[:, j * P:(j + 1) * P], tile(src, par, j), ident[:, :])
                last.then_inc(done, 1)

            def half(k, g0, q):
                r, t, h = k % RING, k // 2, k % 2
                if g0 >= 1 or k >= RING:
                    pe.wait_ge(e_used[r], 2 * g0 + k // RING + 2 * q)
                cols = slice(4 * h * P, (4 * h + 4) * P)
                hi, lo = tile(h2_hi, g0 % 2, t), tile(h2_lo, g0 % 2, t)
                mm(ring[r][:, :], hi, expert_w_hi[:, cols], start=True, stop=False)
                mm(ring[r][:, :], hi, expert_w_lo[:, cols], start=False, stop=False)
                mm(ring[r][:, :], lo, expert_w_hi[:, cols], start=False, stop=True).then_inc(e_ready[r], 1)

            def step(s, i):
                q = SLOTS * i
                g2, g1, g0, gt = s + 2, s + 1, s, s - 1
                bq = (SLOTS // per_batch) * i
                A, B, E, T = 0 <= g2 < groups, 0 <= g1 < groups, 0 <= g0 < groups, 0 <= gt < groups
                if s == -2:
                    gate_rows()
                if s == 0:
                    pe.wait_ge(lo_ready, 1)
                    pe.wait_ge(outw_ready, 1)
                    pe.wait_ge(gb_ready, 1)
                if A:
                    pe.wait_ge(h1_ready, g2 + 1 + q)
                    if g2 == 0:
                        pe.wait_ge(early_in, 16 * 6)
                        pe.wait_ge(v_bias_ready, 1)
                    if g0 >= 1:
                        pe.wait_ge(mix_ready, g0 + q)
                    mm(bank_v[:, :], b_v_parts[:, :], ones_bf[:, :], start=True, stop=False)
                    mm(bank_v[:, :], w_in[:, 0:P], h1_t[:, g2 % 2, :], start=False,
                       stop=True).then_inc(v_ready, 1)
                    if g0 >= 1:
                        pe.wait_ge(wt_copied, g0 + q)
                    mm(bank_g[:, :], w_in[:, P:2 * P], h1_t[:, g2 % 2, :], start=True,
                       stop=True).then_inc(g_ready, 1)
                if E:
                    pe.wait_ge(h2_split, g0 + 1 + q)
                    half(0, g0, q)
                    half(1, g0, q)
                    half(2, g0, q)
                if B:
                    pe.wait_ge(xn2_ready, g1 + 1 + q)
                    if g1 >= 1:
                        pe.wait_ge(sub_ready, g1 + q)
                    turn(bank_b, xn2, g1 % 2, x1t_ready)
                if T:
                    pe.wait_ge(wt_copied, gt + 1 + q)
                    if gt == 0:
                        pe.wait_ge(bias_parts_ready, 1)
                    if A:
                        pe.wait_ge(scan_done, g2 + 1 + q)
                    else:
                        pe.wait_ge(mix_ready, gt + 1)
                    mm(bank_v[:, :], w_parts_t[:, gt % 2, :], expert_b_parts[:, :], start=True,
                       stop=True).then_inc(bias_ready, 1)
                if A:
                    pe.wait_ge(y_ready, g2 + 1 + q)
                    if g2 == 0:
                        pe.wait_ge(outw_ready, 1)
                    b = g2 // per_batch + bq
                    mm(bank_a[:, :], pick_bf[:, bass.ds(b, 1), :].rearrange("p b n -> p (b n)"),
                       gab_parts[:, :].unsqueeze(1).to_broadcast([3 * PART, TILES, P]),
                       start=True, stop=False)
                    for j in range(TILES):
                        last = mm(bank_a[:, j * P:(j + 1) * P], tile(y_t, g2 % 2, j),
                                  w_outg[:, bass.ds(b, 1), :].rearrange("p b n -> p (b n)"),
                                  start=False, stop=(j == TILES - 1))
                    last.then_inc(o_ready, 1)
                if E:
                    half(3, g0, q)
                if B:
                    pe.wait_ge(h2_ready, g1 + 1 + q)
                    if g1 == 0:
                        pe.wait_ge(gate_b_ready, 1)
                    mm(bank_b[:, 0:TE], ones_bf[:, 0:P], gate_b_parts[:, :], start=True, stop=False)
                    for j in range(TILES):
                        last = mm(bank_b[:, j * experts:(j + 1) * experts], tile(h2_t, g1 % 2, j),
                                  gate_w[:, :], start=False, stop=(j == TILES - 1))
                    last.then_inc(logit_ready, 1)
                if E:
                    half(4, g0, q)
                if 0 <= g2 + 1 < groups:
                    pe.wait_ge(xn1_ready, g2 + 2 + q)
                    if g2 >= 0:
                        pe.wait_ge(x1_ready, g2 + 1 + q)
                    turn(bank_a, xn1, (g2 + 1) % 2, xt_ready)
                if E:
                    half(5, g0, q)
                    pe.wait_ge(wp_ready, g0 + 1 + q)
                    pe.wait_ge(gate_done, min(g2 + 1, groups) + q)
                    nc.tensor.transpose(bank_g[0:3 * TE, 0:P],
                                        w_parts[:, :, :].bitcast(F32).rearrange("p a b -> p (a b)"),
                                        ident[:, :]).then_inc(wt_ready, 1)
                    half(6, g0, q)
                    half(7, g0, q)

            steps(pe, step, -3, groups)


_INS = ["L0_attn_x", "L0_attn_W_in", "L0_attn_b_in", "L0_attn_A", "L0_attn_C", "L0_attn_W_out",
        "L0_attn_b_out", "L0_ffn_gate_w", "L0_ffn_gate_b", "L0_ffn_expert_w", "L0_ffn_expert_b",
        "L0_c", "L0_wmod"]
_OUTS = [((8, 1024, 128), "float32")]


def kernel(**inputs):
    import numpy as _np
    import concourse.bacc as _bacc
    from concourse import mybir as _mybir
    from concourse.bass_utils import run_bass_kernel_spmd as _run

    nc = _bacc.Bacc("TRN2", target_bir_lowering=False, num_devices=1)
    arrays, args = {}, []
    for name in _INS:
        a = _np.ascontiguousarray(inputs[name])
        arrays[f"in_{name}_dram"] = a
        args.append(nc.dram_tensor(f"in_{name}_dram", a.shape, _mybir.dt.from_np(a.dtype), kind="ExternalInput").ap())
    for i, (shape, dtype) in enumerate(_OUTS):
        dt = _mybir.dt.from_np(_np.dtype(dtype))
        args.append(nc.dram_tensor(f"out_{i}_dram", shape, dt, kind="ExternalOutput").ap())
    adaln_kernel(nc, *args)
    r = _run(nc, [arrays], core_ids=[0])
    return r.results[0]["out_0_dram"]
```

```python
from contextlib import ExitStack

import concourse.bass as bass
from concourse import mybir

I32 = mybir.dt.int32
F32 = mybir.dt.float32
F32R = mybir.dt.float32r
BF16 = mybir.dt.bfloat16
ALU = mybir.AluOpType
ACT = mybir.ActivationFunctionType
AX = mybir.AxisListType

P = 128
TILES = 4
GROUP = TILES * P
LN_EPS = 1e-5
THRESHOLD = 0.1
GATE_FLOOR = 0.25
RSQRT_SEED = float(0x5F1FFFF9)
RSQRT_C, RSQRT_D = 0.703952253, 2.38924456
LAST_SCALE = 0.375
SLOTS = 4
RING = 4
HALVES = 8
DVE_HALF = 7
PART = 32


def adaln_kernel(nc, x_d, w_in_d, b_in_d, a_d, c_skip_d, w_out_d, b_out_d, gate_w_d, gate_b_d,
                 expert_w_d, expert_b_d, cond_d, wmod_d, out_d):
    batches, seq, d = x_d.shape
    experts = gate_w_d.shape[1]
    groups = batches * seq // GROUP
    per_batch = seq // GROUP
    assert d == P and experts == 8 and per_batch == 2 and groups % SLOTS == 0
    TE = TILES * experts
    first_looped, looped = 1, groups - SLOTS

    x_g = x_d.rearrange("b t d -> (b t) d").rearrange("(g j p) d -> g p j d", j=TILES, p=P)
    out_g = out_d.rearrange("b t d -> (b t) d").rearrange("(g j p) d -> g p j d", j=TILES, p=P)

    with ExitStack() as ctx:
        def sb(name, shape, dt=F32):
            return ctx.enter_context(nc.sbuf_tensor(name, shape, dt))

        def bank(name):
            return ctx.enter_context(nc.psum_tensor(name, [P, 512], F32))

        def sem(name):
            return ctx.enter_context(nc.semaphore(name))

        ident = sb("ident", [P, P])
        w_in = sb("w_in", [P, 2 * P])
        wmod = sb("wmod", [P, 6 * P])
        w_out = sb("w_out", [P, P])
        w_outc = sb("w_outc", [P, P])
        w_outg = sb("w_outg", [P, batches, P])
        gate_w = sb("gate_w", [P, experts])
        gate_b = sb("gate_b", [1, TE])
        expert_w = sb("expert_w", [P, experts * P])
        expert_w_hi = sb("expert_w_hi", [P, experts * P], F32R)
        expert_w_lo = sb("expert_w_lo", [P, experts * P], F32R)
        expert_b = sb("expert_b", [3 * TE, TILES * P])
        expert_b_parts = sb("expert_b_parts", [3 * TE, TILES * P], F32R)
        cond = sb("cond", [batches, P])
        cond_tanh = sb("cond_tanh", [batches, P])
        cond_silu2 = sb("cond_silu2", [batches, P])
        silu_t = sb("silu_t", [P, batches])
        mod_cols = sb("mod_cols", [P, 4, batches])
        a_col = sb("a_col", [P, 1])
        c_col = sb("c_col", [P, 1])
        c_half = sb("c_half", [P, 1])
        b_gate = sb("b_gate", [P, 1])
        b_gate_half = sb("b_gate_half", [P, 1])
        decay = sb("decay", [P, 1])
        a_tanh = sb("a_tanh", [P, 1])
        b_v_row = sb("b_v_row", [1, P])
        b_out_row = sb("b_out_row", [batches, P])
        pick_bf = sb("pick_bf", [3 * PART, batches, P], BF16)
        gab_rows = sb("gab_rows", [batches, P])
        gab_mid = sb("gab_mid", [batches, P])
        gab_parts = sb("gab_parts", [3 * PART, P], BF16)
        b_v_parts = sb("b_v_parts", [PART + 1, P], F32R)
        ones = sb("ones", [PART + 1, GROUP], F32R)
        pick = sb("pick", [PART + batches, batches, P], F32R)
        g_parts = sb("g_parts", [PART + batches, 2 * P], F32R)
        g_abs = sb("g_abs", [batches, 2 * P])
        g_sign = sb("g_sign", [batches, 2 * P])
        g_rows = sb("g_rows", [batches, 2 * P])
        gb_all = sb("gb_all", [P, batches, P])

        x_in = sb("x_in", [P, SLOTS, GROUP])
        x1 = sb("x1", [P, SLOTS, GROUP])
        xn1 = sb("xn1", [P, 2, GROUP])
        xn2 = sb("xn2", [P, 2, GROUP])
        h1_t = sb("h1_t", [P, 2, GROUP])
        h2_t = sb("h2_t", [P, 2, GROUP])
        h2_hi = sb("h2_hi", [P, 2, GROUP], F32R)
        h2_lo = sb("h2_lo", [P, 2, GROUP], F32R)
        hs = sb("hs", [P, 2, GROUP])
        gate_th = sb("gate_th", [P, 2, GROUP])
        y_t = sb("y_t", [P, 2, GROUP])
        bn1 = sb("bn1", [P, 2, TILES, 6])
        bn2 = sb("bn2", [P, TILES, 6])
        mean_var = sb("mean_var", [P, 2 * TILES, 2])
        var_e = sb("var_e", [P, 2 * TILES])
        neg_mean = sb("neg_mean", [P, 2, 2 * TILES])
        half_bits = sb("half_bits", [P, 2 * TILES], I32)
        guess = sb("guess", [P, 2 * TILES])
        guess_t = sb("guess_t", [P, 2 * TILES])
        rstd = sb("rstd", [P, 2, 2 * TILES])
        l_max = sb("l_max", [P, TILES])
        l_sub = sb("l_sub", [P, TILES, experts])
        l_exp = sb("l_exp", [P, TILES, experts])
        l_sum = sb("l_sum", [P, TILES])
        keep = sb("keep", [P, TILES, experts])
        w_sum = sb("w_sum", [P, TILES])
        w_inv = sb("w_inv", [P, TILES])
        w_kept = sb("w_kept", [P, TILES, experts])
        wts = sb("wts", [P, 2, TILES, experts])
        w_parts = sb("w_parts", [P, 3, TE], F32R)
        w_parts_t = sb("w_parts_t", [3 * TE, 2, P], F32R)
        z = sb("z", [P, 2, TILES, experts, P])
        mix = sb("mix", [P, 2, TILES, P])
        mix_g = sb("mix_g", [P, 2, TILES, P])

        ring = [bank(f"ring{r}") for r in range(RING)]
        bank_a = bank("bank_a")
        bank_b = bank("bank_b")
        bank_v = bank("bank_v")
        bank_g = bank("bank_g")

        cond_in = sem("cond_in")
        wmod_in = sem("wmod_in")
        b_v_in = sem("b_v_in")
        w_in_in = sem("w_in_in")
        vectors_in = sem("vectors_in")
        w_out_in = sem("w_out_in")
        late_in = sem("late_in")
        bias_in = sem("bias_in")
        zeroed = sem("zeroed")
        ident_ready = sem("ident_ready")
        lo_ready = sem("lo_ready")
        tanh_ready = sem("tanh_ready")
        silu_ready = sem("silu_ready")
        hi_ready = sem("hi_ready")
        gb_ready = sem("gb_ready")
        picks_ready = sem("picks_ready")
        gate_parts_ready = sem("gate_parts_ready")
        silu2_ready = sem("silu2_ready")
        mod_ready = sem("mod_ready")
        guarded = sem("guarded")
        v_bias_ready = sem("v_bias_ready")
        gab_ready = sem("gab_ready")
        outw_ready = sem("outw_ready")
        bias_parts_ready = sem("bias_parts_ready")
        prep_step = sem("prep_step")
        pool_prep_step = sem("pool_prep_step")
        silu_t_done = sem("silu_t_done")
        mod_done = sem("mod_done")
        gates_done = sem("gates_done")
        x_first = [sem(f"x_first{g}") for g in range(SLOTS)]
        x_loaded = sem("x_loaded")
        x_ready = sem("x_ready")
        bn1_done = sem("bn1_done")
        bn2_done = sem("bn2_done")
        stats_done = sem("stats_done")
        root_step = sem("root_step")
        rstd_ready = sem("rstd_ready")
        xn1_ready = sem("xn1_ready")
        xn2_ready = sem("xn2_ready")
        xt_ready = sem("xt_ready")
        h1_ready = sem("h1_ready")
        v_ready = sem("v_ready")
        g_ready = sem("g_ready")
        scan_done = sem("scan_done")
        gate_done = sem("gate_done")
        y_ready = sem("y_ready")
        o_ready = sem("o_ready")
        x1_ready = sem("x1_ready")
        x1t_ready = sem("x1t_ready")
        h2_made = sem("h2_made")
        h2_ready = sem("h2_ready")
        h2_split = sem("h2_split")
        logit_ready = sem("logit_ready")
        router_step = sem("router_step")
        sub_ready = sem("sub_ready")
        exp_ready = sem("exp_ready")
        w_ready = sem("w_ready")
        hi_part_ready = sem("hi_part_ready")
        wp_ready = sem("wp_ready")
        wt_ready = sem("wt_ready")
        wt_copied = sem("wt_copied")
        bias_ready = sem("bias_ready")
        e_ready = [sem(f"e_ready{r}") for r in range(RING)]
        e_used = [sem(f"e_used{r}") for r in range(RING)]
        pair_added = sem("pair_added")
        mix_step = sem("mix_step")
        mix_ready = sem("mix_ready")
        mixg_ready = sem("mixg_ready")
        out_ready = sem("out_ready")
        last_ready = sem("last_ready")
        last_step = sem("last_step")
        out_sent = sem("out_sent")
        x1_free = sem("x1_free")

        block = ctx.enter_context(nc.Block())

        def steps(eng, step, first, last):
            for s in range(first, first_looped):
                step(s, 0)
            with eng.Fori(0, looped // SLOTS) as i:
                for s in range(first_looped, first_looped + SLOTS):
                    step(s, i)
            for s in range(first_looped + looped, last + 1):
                step(s, 0)

        def wait_apart(eng, *waits):
            waits = [(semaphore, v if isinstance(v, int) else eng.to_reg(v)) for semaphore, v in waits]
            eng.wait_ge(ident_ready, 1)
            for semaphore, value in waits:
                eng.wait_ge(semaphore, value)

        def split_rows(ops, prep, src, dst, n):
            prep(ops.tensor_copy(dst[0:n, :], src))
            return ops.tensor_tensor(dst[PART:PART + n, :], src, dst[0:n, :].bitcast(F32), ALU.subtract)

        def split_rows_bf(ops, prep, src, rest, mid, dst, n):
            prep(ops.tensor_copy(dst[0:n, :], src))
            prep(ops.tensor_tensor(rest, src, dst[0:n, :], ALU.subtract))
            prep(ops.tensor_copy(dst[PART:PART + n, :], rest))
            prep(ops.tensor_copy(mid, dst[PART:PART + n, :]))
            prep(ops.tensor_tensor(rest, rest, mid, ALU.subtract))
            return ops.tensor_copy(dst[2 * PART:2 * PART + n, :], rest)

        def one_hot():
            return ident[0:batches, 0:batches].unsqueeze(2).to_broadcast([batches, batches, P])

        def logit_bank(g):
            return bank_a if g == groups - 1 else bank_b

        def tile(buf, slot, j):
            return buf[:, slot, j * P:(j + 1) * P]

        def by_tile(ap):
            return ap.rearrange("p (j n) -> p j n", j=TILES)

        def slot_of(buf, g):
            if isinstance(g, int):
                return by_tile(buf[:, g % SLOTS, :])
            return buf[:, bass.ds(g % SLOTS, 1), :].rearrange("p s (j n) -> p (s j) n", j=TILES)

        @block.sync
        def _(sp):
            def arrived(g):
                sp.wait_ge(x_loaded, 16 * (g + 1 - SLOTS))
                sp.sem_inc(x_ready, 1)

            def refill(g):
                wait_apart(sp, (x1_ready, g + 1))
                sp.dma_start(slot_of(x_in, g), x_g[g + SLOTS]).then_inc(x_loaded, 16)
                arrived(g + SLOTS)

            def store(g):
                wait_apart(sp, (out_ready, g + 1))
                sp.dma_start(out_g[g], slot_of(x1, g)).then_inc(out_sent, 16)
                sp.wait_ge(out_sent, 16 * (g + 1))
                sp.sem_inc(x1_free, 1)

            def first_load(g):
                sp.dma_start(slot_of(x_in, g), x_g[g]).then_inc(x_first[g], 16)

            sp.dma_start(cond[:, :], cond_d).then_inc(cond_in, 16)
            sp.dma_start(b_v_row[:, :], b_in_d[0:P].rearrange("(o n) -> o n", o=1)).then_inc(b_v_in, 16)
            first_load(0)
            sp.dma_start(wmod[:, :], wmod_d).then_inc(wmod_in, 16)
            first_load(1)
            sp.dma_start(w_in[:, :], w_in_d).then_inc(w_in_in, 16)
            sp.dma_start(w_out[:, :], w_out_d).then_inc(w_out_in, 16)
            first_load(2)
            first_load(3)
            sp.sem_inc(x1_free, SLOTS)
            sp.sem_inc(mix_ready, 1)
            for g in range(SLOTS):
                sp.wait_ge(x_first[g], 16)
                sp.sem_inc(x_ready, 1)
                if g == 1:
                    sp.wait_ge(zeroed, 3)
                    for part in range(3):
                        for t in range(TILES):
                            r = part * TE + t * experts
                            sp.dma_start(expert_b[r:r + experts, t * P:(t + 1) * P],
                                         expert_b_d).then_inc(bias_in, 16)
            head = 4
            for g in range(head):
                refill(g)
            with sp.Fori(0, groups - SLOTS - head) as g:
                store(g)
                refill(g + head)
            sp.sem_inc(x_ready, 2)
            with sp.Fori(groups - SLOTS - head, groups - 1) as g:
                store(g)
            sp.wait_ge(last_ready, 2)
            sp.dma_start(out_g[groups - 1], slot_of(x1, groups - 1)).then_inc(out_sent, 16)
            sp.wait_ge(out_sent, 16 * groups)

        @block.gpsimd
        def _(pool):
            made = [0]

            def prep(ins):
                made[0] += 1
                ins.then_inc(pool_prep_step, 1)
                pool.wait_ge(pool_prep_step, made[0])

            prep(nc.gpsimd.memset(ident[:, :], 0.0))
            nc.gpsimd.affine_select(out=ident[:, :], in_=ident[:, :], compare_op=ALU.not_equal,
                                    fill=1.0, base=0, pattern=[[-1, P]],
                                    channel_multiplier=1).then_inc(ident_ready, 1)
            nc.gpsimd.memset(pick_bf[:, :, :], 0.0).then_inc(zeroed, 1)
            nc.gpsimd.memset(pick[:, :, :].bitcast(F32), 0.0).then_inc(zeroed, 1)
            nc.gpsimd.memset(expert_b[:, :], 0.0).then_inc(zeroed, 1)
            nc.gpsimd.memset(gab_parts[:, :], 0.0)
            for rows in (b_v_parts, g_parts):
                nc.gpsimd.memset(rows[:, :].bitcast(F32), 0.0)
            nc.gpsimd.memset(ones[:, :].bitcast(F32), 1.0).then_inc(zeroed, 1)
            pool.wait_ge(zeroed, 4)
            pool.wait_ge(b_v_in, 16)
            split_rows(nc.gpsimd, prep, b_v_row[:, :], b_v_parts, 1).then_inc(v_bias_ready, 1)
            pool.wait_ge(v_bias_ready, 1)

            def gab():
                pool.wait_ge(vectors_in, 16 * 5)
                pool.wait_ge(guarded, 1)
                prep(nc.gpsimd.tensor_tensor(gab_rows[:, :], g_rows[:, 0:P], b_out_row[:, :], ALU.mult))
                split_rows_bf(nc.gpsimd, prep, gab_rows[:, :], gab_rows[:, :], gab_mid[:, :], gab_parts,
                              batches).then_inc(gab_ready, 1)
                pool.wait_ge(gab_ready, 1)

            def norm(src, slot_src, dst, pair, col):
                for j in range(TILES):
                    last = nc.gpsimd.tensor_scalar(
                        tile(dst, pair % 2, j), tile(src, slot_src, j),
                        neg_mean[:, pair % 2, col + j:col + j + 1],
                        rstd[:, pair % 2, col + j:col + j + 1], ALU.add, ALU.mult)
                return last

            def fold(g, t, q):
                for k in (2 * t, 2 * t + 1):
                    pool.wait_ge(e_used[k % RING], 2 * g + k // RING + 1 + 2 * q)
                nc.gpsimd.tensor_tensor(z[:, g % 2, t, 0:4, :], z[:, g % 2, t, 0:4, :],
                                        z[:, g % 2, t, 4:8, :], ALU.add).then_inc(pair_added, 1)

            def weight_parts(g, q):
                w = wts[:, g % 2].rearrange("p j e -> p (j e)")
                if g >= 1:
                    wait_apart(pool, (w_ready, g + 1 + q), (wt_ready, g + q))
                else:
                    pool.wait_ge(w_ready, g + 1)
                nc.gpsimd.tensor_copy(w_parts[:, 0:3:2, :], w.unsqueeze(1).to_broadcast([P, 2, TE])) \
                    .then_inc(hi_part_ready, 1)
                wait_apart(pool, (hi_part_ready, g + 1 + q))
                nc.gpsimd.tensor_tensor(w_parts[:, 1, :], w, w_parts[:, 0, :].bitcast(F32),
                                        ALU.subtract).then_inc(wp_ready, 1)

            def norm2(g1, q):
                if g1 >= 2:
                    wait_apart(pool, (rstd_ready, g1 + 3 + q), (x1t_ready, g1 - 1 + q))
                else:
                    pool.wait_ge(rstd_ready, g1 + 3)
                norm(x1, g1 % SLOTS, xn2, g1, 0).then_inc(xn2_ready, 1)

            def times_gb(gt, q, b, tiles=TILES):
                wait_apart(pool, (mix_ready, gt + 2 + q))
                if gt == 0:
                    pool.wait_ge(gb_ready, 1)
                nc.gpsimd.tensor_tensor(
                    mix_g[:, gt % 2, 0:tiles, :], mix[:, gt % 2, 0:tiles, :],
                    gb_all[:, bass.ds(b, 1), :].to_broadcast([P, tiles, P]),
                    ALU.mult).then_inc(mixg_ready, 1)

            def add_pairs(g, *waits):
                for semaphore, value in waits:
                    pool.wait_ge(semaphore, value)
                nc.gpsimd.tensor_tensor(z[:, g % 2, 0:2, 0:2, :], z[:, g % 2, 0:2, 0:2, :],
                                        z[:, g % 2, 0:2, 2:4, :], ALU.add).then_inc(pair_added, 1)

            def step(s, i):
                q = SLOTS * i
                g1, g0, gt = s + 1, s, s - 1
                E, T = 0 <= g0 < groups, 0 <= gt < groups
                if g1 < 0:
                    pool.wait_ge(rstd_ready, g1 + 3)
                else:
                    norm2(g1, q)
                if T:
                    fold(gt, 2, q)
                if 0 <= g1 + 2 < groups:
                    if g1 >= 0:
                        wait_apart(pool, (xt_ready, g1 + 1 + q))
                    norm(x_in, (g1 + 2) % SLOTS, xn1, g1, TILES).then_inc(xn1_ready, 1)
                if E:
                    weight_parts(g0, q)
                    fold(g0, 0, q)
                    fold(g0, 1, q)
                if T:
                    times_gb(gt, q, gt // per_batch + (SLOTS // per_batch) * i)
                if g1 == groups - 2:
                    norm2(groups - 1, 0)
                if E:
                    add_pairs(g0, (pair_added, 4 * g0 + 2 + 4 * q))
                if s == -3:
                    gab()
                if s == -2:
                    pool.wait_ge(hi_ready, 1)
                    nc.gpsimd.tensor_tensor(expert_w_lo[:, :], expert_w[:, :],
                                            expert_w_hi[:, :].bitcast(F32),
                                            ALU.subtract).then_inc(lo_ready, 1)

            def ending():
                a, b, c = groups - 3, groups - 2, groups - 1
                fold(a, 2, 0)
                weight_parts(b, 0)
                fold(b, 1, 0)
                add_pairs(b, (e_used[1], 2 * b + 1), (pair_added, 4 * b + 1))
                weight_parts(c, 0)
                times_gb(a, 0, a // per_batch)
                fold(c, 0, 0)
                times_gb(b, 0, b // per_batch)
                add_pairs(c, (pair_added, 4 * b + 3), (e_used[3], 2 * c + 1))
                pool.wait_ge(mixg_ready, b + 1)
                nc.gpsimd.tensor_tensor(x1[:, b % SLOTS, :], mix_g[:, b % 2].rearrange("p j n -> p (j n)"),
                                        x1[:, b % SLOTS, :], ALU.add).then_inc(out_ready, 1)
                times_gb(c, 0, c // per_batch, 2)
                pool.wait_ge(mixg_ready, c + 1)
                nc.gpsimd.tensor_tensor(x1[:, c % SLOTS, 0:2 * P],
                                        mix_g[:, c % 2, 0:2, :].rearrange("p j n -> p (j n)"),
                                        x1[:, c % SLOTS, 0:2 * P], ALU.add).then_inc(last_ready, 1)

            steps(pool, step, -3, groups - 3)
            ending()

        @block.scalar
        def _(act):
            def column(v):
                return v.rearrange("(p o) -> p o", o=1)

            def row(v):
                return v.rearrange("(o n) -> o n", o=1)

            act.wait_ge(cond_in, 16)
            nc.scalar.activation(cond_tanh[:, :], cond[:, :], ACT.Tanh, scale=0.5).then_inc(tanh_ready, 1)
            act.wait_ge(silu_t_done, 1)
            nc.scalar.mul(silu_t[:, :], bank_a[:, 0:batches], 0.5).then_inc(silu_ready, 1)
            act.wait_ge(zeroed, 2)
            for part in range(2):
                last = nc.scalar.copy(pick[PART * part:PART * part + batches, :, :], one_hot())
            last.then_inc(picks_ready, 1)
            act.dma_start(a_col[:, :], column(a_d)).then_inc(vectors_in, 16)
            act.dma_start(b_gate[:, :], column(b_in_d[P:2 * P])).then_inc(vectors_in, 16)
            act.dma_start(c_col[:, :], column(c_skip_d)).then_inc(vectors_in, 16)
            act.dma_start(b_out_row[:, :], row(b_out_d).to_broadcast([batches, P])).then_inc(vectors_in, 16)
            act.dma_start(gate_b[:, :].rearrange("o (j e) -> o j e", j=TILES),
                          row(gate_b_d).unsqueeze(1).to_broadcast([1, TILES, experts])).then_inc(vectors_in, 16)
            act.dma_start(gate_w[:, :], gate_w_d).then_inc(late_in, 16)
            for h in range(2):
                act.dma_start(
                    expert_w[:, h * 512:(h + 1) * 512].rearrange("p (e n) -> p e n", e=4),
                    expert_w_d[4 * h:4 * h + 4].rearrange("e d n -> d e n")).then_inc(late_in, 16)
            act.wait_ge(vectors_in, 16 * 5)
            nc.scalar.activation(a_tanh[:, :], a_col[:, :], ACT.Tanh, scale=0.5)
            nc.scalar.mul(b_gate_half[:, :], b_gate[:, :], 0.5)
            nc.scalar.mul(c_half[:, :], c_col[:, :], 0.5).then_inc(tanh_ready, 1)
            def late_prep():
                act.wait_ge(late_in, 16 * 3)
                nc.scalar.copy(expert_w_hi[:, :], expert_w[:, :]).then_inc(hi_ready, 1)
                act.wait_ge(bias_in, 16 * 3 * TILES)
                nc.scalar.copy(expert_b_parts[:, :], expert_b[:, :]).then_inc(hi_ready, 1)

            def gb_copy():
                act.wait_ge(outw_ready, 1)
                for h in range(RING):
                    last = nc.scalar.copy(
                        gb_all[:, 2 * h:2 * h + 2, :],
                        ring[h][:, :].rearrange("p (b k n) -> p b k n", b=2, k=2)[:, :, 1, :])
                last.then_inc(gb_ready, 1)

            def mod(k, b):
                return mod_cols[:, k, bass.ds(b, 1)]

            def weigh(g0, k, q):
                r, t, h = k % RING, k // 2, k % 2
                act.wait_ge(e_ready[r], 2 * g0 + k // RING + 1 + 2 * q)
                for e in range(4 * h, 4 * h + 4):
                    last = nc.scalar.activation(
                        z[:, g0 % 2, t, e, :], ring[r][:, (e % 4) * P:(e % 4 + 1) * P], ACT.Copy,
                        scale=wts[:, g0 % 2, t, e:e + 1])
                last.then_inc(e_used[r], 1)

            def second_h(g1, q, b):
                if g1 >= 2:
                    wait_apart(act, (x1t_ready, g1 + 1 + q), (h2_split, g1 - 1 + q),
                               (e_ready[RING - 1], 2 * g1 - 2 + 2 * q))
                else:
                    act.wait_ge(x1t_ready, g1 + 1)
                nc.scalar.activation(h2_t[:, g1 % 2, :], bank_b[:, :], ACT.Identity,
                                     bias=mod(2, b), scale=mod(3, b)).then_inc(h2_made, 1)
                nc.scalar.activation(h2_hi[:, g1 % 2, :], bank_b[:, :], ACT.Identity,
                                     bias=mod(2, b), scale=mod(3, b)).then_inc(h2_ready, 1)

            def parts_out(g0, q):
                act.wait_ge(wt_ready, g0 + 1 + q)
                nc.scalar.copy(w_parts_t[:, g0 % 2, :], bank_g[0:3 * TE, 0:P]).then_inc(wt_copied, 1)

            def exponentials(g, q):
                act.wait_ge(sub_ready, g + 1 + q)
                nc.scalar.activation(l_exp[:, :, :], l_sub[:, :, :], ACT.Exp).then_inc(exp_ready, 1)

            def step(s, i):
                q = SLOTS * i
                g2, g1, g0, gt = s + 2, s + 1, s, s - 1
                bq = (SLOTS // per_batch) * i
                A, B, E, T = 0 <= g2 < groups, 0 <= g1 < groups, 0 <= g0 < groups, 0 <= gt < groups
                if s == -2:
                    late_prep()
                if T:
                    weigh(gt, 6, q)
                if A:
                    act.wait_ge(g_ready, g2 + 1 + q)
                    if g2 >= 2:
                        act.wait_ge(y_ready, g2 - 1 + q)
                    nc.scalar.activation(gate_th[:, g2 % 2, :], bank_g[:, :], ACT.Tanh,
                                         bias=b_gate_half[:, 0:1], scale=0.5).then_inc(gate_done, 1)
                if E:
                    act.wait_ge(w_ready, g0 + 1 + q)
                    weigh(g0, 0, q)
                if B:
                    second_h(g1, q, g1 // per_batch + bq)
                if E:
                    for k in range(1, 4):
                        weigh(g0, k, q)
                if 0 <= g2 + 1 < groups:
                    if g2 + 1 == 0:
                        act.wait_ge(mod_ready, 1)
                    if g2 >= 1:
                        wait_apart(act, (xt_ready, g2 + 2 + q), (g_ready, g2 + q))
                    else:
                        act.wait_ge(xt_ready, g2 + 2)
                    b = (g2 + 1) // per_batch + bq
                    nc.scalar.activation(h1_t[:, (g2 + 1) % 2, :], (bank_b if s == -2 else bank_a)[:, :],
                                         ACT.Identity,
                                         bias=mod(0, b), scale=mod(1, b)).then_inc(h1_ready, 1)
                if s == -2:
                    gb_copy()
                if E:
                    weigh(g0, 4, q)
                    parts_out(g0, q)
                    weigh(g0, 5, q)
                if B:
                    exponentials(g1, q)

            def ending():
                a, b, c = groups - 3, groups - 2, groups - 1
                weigh(a, 6, 0)
                act.wait_ge(w_ready, b + 1)
                weigh(b, 0, 0)
                second_h(c, 0, c // per_batch)
                weigh(b, 2, 0)
                exponentials(c, 0)
                weigh(b, 3, 0)
                parts_out(b, 0)
                weigh(b, 4, 0)
                weigh(b, 6, 0)
                act.wait_ge(w_ready, c + 1)
                weigh(c, 0, 0)
                weigh(c, 2, 0)
                weigh(c, 1, 0)
                parts_out(c, 0)
                weigh(c, 4, 0)
                weigh(c, 6, 0)

            steps(act, step, -3, groups - 3)
            ending()

        @block.vector
        def _(dve):
            vec = nc.vector
            made = [0]

            def prep(ins):
                made[0] += 1
                ins.then_inc(prep_step, 1)
                dve.wait_ge(prep_step, made[0])

            def picks():
                dve.wait_ge(zeroed, 1)
                for part in range(3):
                    last = vec.tensor_copy(pick_bf[PART * part:PART * part + batches, :, :], one_hot())
                last.then_inc(picks_ready, 1)

            def modulation():
                dve.wait_ge(mod_done, 1)
                for k, plus in ((0, 0.0), (1, 1.0), (2, 0.0), (3, 1.0)):
                    last = vec.tensor_scalar(mod_cols[:, k, :], bank_b[:, k * batches:(k + 1) * batches],
                                             plus, None, ALU.add)
                last.then_inc(mod_ready, 1)
                dve.wait_ge(mod_done, 2)
                rows = bank_v[0:batches, 0:2 * P]
                prep(vec.tensor_scalar(g_sign[:, :], rows, 0.0, 2.0, ALU.is_ge, ALU.mult))
                prep(vec.tensor_scalar(g_sign[:, :], g_sign[:, :], -1.0, None, ALU.add))
                prep(vec.tensor_tensor(g_abs[:, :], g_sign[:, :], rows, ALU.mult))
                vec.scalar_tensor_tensor(out=g_rows[:, :], in0=g_abs[:, :], scalar=GATE_FLOOR,
                                         in1=g_sign[:, :], op0=ALU.max, op1=ALU.mult).then_inc(guarded, 1)
                dve.wait_ge(guarded, 1)
                dve.wait_ge(zeroed, 4)
                split_rows(vec, prep, g_rows[:, :], g_parts, batches).then_inc(gate_parts_ready, 1)

            def decay_and_c():
                dve.wait_ge(w_out_in, 16)
                dve.wait_ge(tanh_ready, 2)
                vec.tensor_scalar(decay[:, :], a_tanh[:, :], 0.5, 0.5, ALU.mult, ALU.add)
                prep(vec.tensor_scalar(w_outc[:, :], w_out[:, :], c_half[:, 0:1], None, ALU.mult))

            def out_weights(h):
                if h == 0:
                    dve.wait_ge(gates_done, 1)
                last = vec.tensor_tensor(
                    w_outg[:, 2 * h:2 * h + 2, :],
                    ring[h][:, :].rearrange("p (b k n) -> p b k n", b=2, k=2)[:, :, 0, :],
                    w_outc[:, :].unsqueeze(1).to_broadcast([P, 2, P]), ALU.mult)
                if h == RING - 1:
                    last.then_inc(outw_ready, 1)

            def bias_parts():
                dve.wait_ge(hi_ready, 2)
                low = slice(2 * TE, 3 * TE)
                vec.tensor_tensor(expert_b_parts[low, :], expert_b[low, :],
                                  expert_b_parts[low, :].bitcast(F32), ALU.subtract) \
                    .then_inc(bias_parts_ready, 1)

            def stats(buf, g, bn, j):
                return vec.bn_stats(bn[:, j, :], tile(buf, g % SLOTS, j))

            ROOT = 9

            def root(n, pair, q):
                par = pair % 2
                if n:
                    dve.wait_ge(root_step, ROOT * (pair + 2) + n + ROOT * q)
                else:
                    dve.wait_ge(stats_done, pair + 3 + q)
                if n == 0:
                    vec.tensor_scalar(neg_mean[:, par, :], mean_var[:, :, 0], -1.0, None, ALU.mult)
                    ins = vec.tensor_scalar(var_e[:, :], mean_var[:, :, 1], LN_EPS, None, ALU.add)
                elif n == 1:
                    ins = vec.tensor_scalar(half_bits[:, :], var_e[:, :].bitcast(I32), 1, None,
                                            ALU.logical_shift_right)
                elif n == 2:
                    ins = vec.tensor_scalar(guess[:, :].bitcast(I32), half_bits[:, :], -1.0, RSQRT_SEED,
                                            ALU.mult, ALU.add)
                elif n == 3:
                    ins = vec.scalar_tensor_tensor(out=guess_t[:, :], in0=guess[:, :],
                                                   scalar=-LAST_SCALE * RSQRT_C, in1=guess[:, :],
                                                   op0=ALU.mult, op1=ALU.mult)
                elif n == 5:
                    ins = vec.scalar_tensor_tensor(out=guess[:, :], in0=guess_t[:, :],
                                                   scalar=LAST_SCALE * RSQRT_C * RSQRT_D, in1=guess[:, :],
                                                   op0=ALU.add, op1=ALU.mult)
                elif n == 6:
                    ins = vec.scalar_tensor_tensor(out=guess_t[:, :], in0=guess[:, :],
                                                   scalar=LAST_SCALE ** -2, in1=guess[:, :],
                                                   op0=ALU.mult, op1=ALU.mult)
                elif n in (4, 7):
                    ins = vec.tensor_tensor(guess_t[:, :], guess_t[:, :], var_e[:, :], ALU.mult)
                elif n == 8:
                    ins = vec.scalar_tensor_tensor(out=guess_t[:, :], in0=guess_t[:, :], scalar=-10.0 / 3.0,
                                                   in1=guess_t[:, :], op0=ALU.add, op1=ALU.mult)
                else:
                    ins = vec.scalar_tensor_tensor(out=rstd[:, par, :], in0=guess_t[:, :], scalar=5.0,
                                                   in1=guess[:, :], op0=ALU.add, op1=ALU.mult)
                ins.then_inc(rstd_ready if n == ROOT else root_step, 1)

            ROUTER, ROUTER_ALL = 6, 8

            def router(n, g, q):
                def before(k):
                    dve.wait_ge(router_step, ROUTER * g + k + ROUTER * q)
                spread = [P, TILES, experts]
                logit = logit_bank(g)[:, 0:TE].rearrange("p (j e) -> p j e", j=TILES)
                if n == 0:
                    dve.wait_ge(logit_ready, g + 1 + q)
                    vec.tensor_reduce(l_max[:, :], logit, AX.X, ALU.max).then_inc(router_step, 1)
                elif n == 1:
                    before(1)
                    vec.tensor_tensor(l_sub[:, :, :], logit,
                                      l_max[:, :].unsqueeze(2).to_broadcast(spread),
                                      ALU.subtract).then_inc(sub_ready, 1)
                elif n == 2:
                    dve.wait_ge(exp_ready, g + 1 + q)
                    vec.tensor_reduce(l_sum[:, :], l_exp[:, :, :], AX.X, ALU.add).then_inc(router_step, 1)
                elif n == 3:
                    before(2)
                    vec.scalar_tensor_tensor(out=keep[:, :, :], in0=l_sum[:, :].unsqueeze(2).to_broadcast(spread),
                                             scalar=THRESHOLD, in1=l_exp[:, :, :],
                                             op0=ALU.mult, op1=ALU.is_le).then_inc(router_step, 1)
                elif n == 4:
                    before(3)
                    vec.tensor_tensor(w_kept[:, :, :], keep[:, :, :], l_exp[:, :, :],
                                      ALU.mult).then_inc(router_step, 1)
                elif n == 5:
                    before(4)
                    vec.tensor_reduce(w_sum[:, :], w_kept[:, :, :], AX.X, ALU.add).then_inc(router_step, 1)
                elif n == 6:
                    before(5)
                    vec.reciprocal(w_inv[:, :], w_sum[:, :]).then_inc(router_step, 1)
                else:
                    before(6)
                    if g >= 2:
                        dve.wait_ge(e_used[2], 2 * g - 2 + 2 * q)
                    vec.tensor_tensor(wts[:, g % 2], w_kept[:, :, :],
                                      w_inv[:, :].unsqueeze(2).to_broadcast(spread),
                                      ALU.mult).then_inc(w_ready, 1)

            def weigh_onto(k, n, g, q):
                if n == 0:
                    count = 2 * g + 1 + k // RING + 2 * q
                    dve.wait_ge(e_ready[k % RING], count)
                    dve.wait_ge(e_used[k % RING - 1], count)
                ins = vec.scalar_tensor_tensor(
                    out=z[:, g % 2, k // 2, n, :], in0=ring[k % RING][:, n * P:(n + 1) * P],
                    scalar=wts[:, g % 2, k // 2, 4 + n:5 + n], in1=z[:, g % 2, k // 2, n, :],
                    op0=ALU.mult, op1=ALU.add)
                if n == 3:
                    ins.then_inc(e_used[k % RING], 1)

            def scan(g, q):
                dve.wait_ge(v_ready, g + 1 + q)
                if g % per_batch:
                    dve.wait_ge(scan_done, g + q)
                vec.tensor_tensor_scan(
                    hs[:, g % 2, :], decay[:, 0:1].to_broadcast([P, GROUP]), bank_v[:, :],
                    hs[:, (g - 1) % 2, GROUP - 1:GROUP] if g % per_batch else 0.0,
                    ALU.mult, ALU.add).then_inc(scan_done, 1)

            def gated(g, q):
                dve.wait_ge(gate_done, g + 1 + q)
                dve.wait_ge(scan_done, g + 1 + q)
                vec.scalar_tensor_tensor(out=y_t[:, g % 2, :], in0=gate_th[:, g % 2, :], scalar=1.0,
                                         in1=hs[:, g % 2, :], op0=ALU.add,
                                         op1=ALU.mult).then_inc(y_ready, 1)

            def sum_pairs(g, count):
                dve.wait_ge(pair_added, count)
                return vec.tensor_tensor(mix[:, g % 2, 0:2, :], z[:, g % 2, 0:2, 0, :],
                                         z[:, g % 2, 0:2, 1, :], ALU.add)

            def sum_fours(g, q, count=None, first=2, last=TILES):
                if count is not None:
                    dve.wait_ge(pair_added, count)
                dve.wait_ge(e_used[3], 2 * g + 2 + 2 * q)
                vec.tensor_reduce(mix[:, g % 2, first:last, :],
                                  z[:, g % 2, first:last, 0:4, :].rearrange("p t e n -> p t n e"),
                                  AX.X, ALU.add).then_inc(mix_step, 1)

            def add_bias(g, q, first=0, last=TILES):
                dve.wait_ge(bias_ready, g + 1 + q)
                dve.wait_ge(mix_step, g + 1 + first + q)
                vec.tensor_tensor(mix[:, g % 2, first:last, :], mix[:, g % 2, first:last, :],
                                  by_tile(bank_v[:, :])[:, first:last, :], ALU.add).then_inc(mix_ready, 1)

            def low_part(g, q):
                dve.wait_ge(h2_ready, g + 1 + q)
                vec.tensor_tensor(h2_lo[:, g % 2, :], h2_t[:, g % 2, :],
                                  h2_hi[:, g % 2, :].bitcast(F32), ALU.subtract).then_inc(h2_split, 1)

            def result(g, q):
                dve.wait_ge(mixg_ready, g + 1 + q)
                vec.tensor_tensor(x1[:, g % SLOTS, :], mix_g[:, g % 2].rearrange("p j n -> p (j n)"),
                                  x1[:, g % SLOTS, :], ALU.add).then_inc(out_ready, 1)

            def share(k, g):
                for n in range(4):
                    weigh_onto(k, n, g, 0)

            def step(s, i):
                q = SLOTS * i
                g2, g1, g0, gt = s + 2, s + 1, s, s - 1
                A, B, E, T = 0 <= g2 < groups, 0 <= g1 < groups, 0 <= g0 < groups, 0 <= gt < groups
                next_norm = 0 <= g2 + 2 < groups
                more_x = 0 <= g2 + 3 < groups

                def x_stats(j):
                    if more_x:
                        if j == 0:
                            dve.wait_ge(x_ready, g2 + 4 + q)
                        ins = stats(x_in, g2 + 3, bn1[:, (g2 + 3) % 2], j)
                        if j == TILES - 1:
                            ins.then_inc(bn1_done, 1)

                if A:
                    gated(g2, q)
                if T:
                    sum_pairs(gt, 4 * gt + 3 + 4 * q)
                    sum_fours(gt, q, 4 * gt + 4 + 4 * q)
                if g1 == 0:
                    bias_parts()
                if A:
                    dve.wait_ge(o_ready, g2 + 1 + q)
                    dve.wait_ge(x1_free, g2 + 1 + q)
                    vec.tensor_tensor(x1[:, g2 % SLOTS, :], bank_a[:, :], x_in[:, g2 % SLOTS, :],
                                      ALU.add).then_inc(x1_ready, 1)
                    dve.wait_ge(x1_ready, g2 + 1 + q)
                    for j in range(TILES):
                        last = stats(x1, g2, bn2, j)
                    last.then_inc(bn2_done, 1)
                stats_after = (-1, 0, 5, 8) if A else (0, 3, 5, 8) if s > -3 else (6, 7, 8, ROOT)
                for j in range(TILES):
                    if stats_after[j] < 0:
                        x_stats(j)
                if A or next_norm:
                    if A:
                        wait_apart(dve, (bn2_done, g2 + 1 + q))
                    else:
                        dve.wait_ge(bn1_done, g2 + 3)
                    for j in range(TILES):
                        if A:
                            last = vec.bn_aggr(mean_var[:, j, :], bn2[:, j, :])
                        if next_norm:
                            last = vec.bn_aggr(mean_var[:, TILES + j, :], bn1[:, g2 % 2, j, :])
                    last.then_inc(stats_done, 1)
                for n in range(ROOT + 1):
                    if A or next_norm:
                        root(n, g2, q)
                    if s == -3 and 2 <= n < 2 + RING:
                        out_weights(n - 2)
                    for j in range(TILES):
                        if n == stats_after[j]:
                            x_stats(j)
                    if n == 1 and T:
                        add_bias(gt, q)
                    if n == 4 and B:
                        low_part(g1, q)
                    if n >= 6 and n < 8 and B:
                        router(n - 6, g1, q)
                if 0 <= g2 + 1 < groups:
                    scan(g2 + 1, q)
                spread_out = g1 < groups - 2
                for n in range(2, ROUTER_ALL):
                    if B:
                        router(n, g1, q)
                    if E and spread_out and 4 <= n < 8:
                        weigh_onto(DVE_HALF, n - 4, g0, q)
                    if n == 3 and T and spread_out:
                        result(gt, q)
                if not spread_out:
                    share(DVE_HALF, g0)
                    result(gt, q)

            def ending():
                a, b, c = groups - 3, groups - 2, groups - 1
                share(1, b)
                low_part(c, 0)
                for n in range(ROUTER_ALL):
                    router(n, c, 0)
                    if n == 1:
                        sum_pairs(a, 4 * a + 3)
                    if n == 2:
                        sum_fours(a, 0, 4 * a + 4)
                add_bias(a, 0)
                share(5, b)
                share(7, b)
                sum_pairs(b, 4 * b + 2)
                sum_fours(b, 0)
                result(a, 0)
                add_bias(b, 0)
                share(3, c)
                share(5, c)
                share(7, c)
                sum_pairs(c, 4 * b + 4).then_inc(mix_step, 1)
                sum_fours(c, 0, first=2, last=3)
                add_bias(c, 0, 0, 2)
                sum_fours(c, 0, first=3)
                add_bias(c, 0, 2, TILES)
                dve.wait_ge(mix_ready, c + 3)
                vec.tensor_tensor(mix_g[:, c % 2, 2:4, :], mix[:, c % 2, 2:4, :],
                                  gb_all[:, c // per_batch:c // per_batch + 1, :].to_broadcast([P, 2, P]),
                                  ALU.mult).then_inc(last_step, 1)
                dve.wait_ge(last_step, 1)
                vec.tensor_tensor(x1[:, c % SLOTS, 2 * P:], mix_g[:, c % 2, 2:4, :].rearrange("p j n -> p (j n)"),
                                  x1[:, c % SLOTS, 2 * P:], ALU.add).then_inc(last_ready, 1)

            vec.memset(mean_var[:, :, :], 1.0)
            dve.wait_ge(cond_in, 16)
            dve.wait_ge(tanh_ready, 1)
            vec.scalar_tensor_tensor(out=cond_silu2[:, :], in0=cond_tanh[:, :], scalar=1.0,
                                     in1=cond[:, :], op0=ALU.add, op1=ALU.mult).then_inc(silu2_ready, 1)
            dve.wait_ge(ident_ready, 1)
            picks()
            step(-5, 0)
            step(-4, 0)
            modulation()
            decay_and_c()
            steps(dve, step, -3, groups - 3)
            ending()

        @block.tensor
        def _(pe):
            mm = nc.tensor.matmul
            pe.wait_ge(ident_ready, 1)
            pe.wait_ge(silu2_ready, 1)
            nc.tensor.transpose(bank_a[:, 0:batches], cond_silu2[:, :],
                                ident[0:batches, 0:batches]).then_inc(silu_t_done, 1)
            pe.wait_ge(silu_ready, 1)
            pe.wait_ge(wmod_in, 16)
            for k, section in enumerate((0, 1, 3, 4)):
                last = mm(bank_b[:, k * batches:(k + 1) * batches],
                          wmod[:, section * P:(section + 1) * P], silu_t[:, :], start=True, stop=True)
            last.then_inc(mod_done, 1)
            for k, section in enumerate((2, 5)):
                last = mm(bank_v[0:batches, k * P:(k + 1) * P], silu_t[:, :],
                          wmod[:, section * P:(section + 1) * P], start=True, stop=True)
            last.then_inc(mod_done, 1)

            def keep_clock(bank_x, n):
                for _ in range(n):
                    mm(bank_x[:, 0:P], ident[:, :], ident[:, :], start=True, stop=True)

            def gate_rows():
                pe.wait_ge(picks_ready, 2)
                pe.wait_ge(gate_parts_ready, 1)
                for b in range(batches):
                    last = mm(ring[b // 2][:, (b % 2) * 2 * P:(b % 2 + 1) * 2 * P], pick[:, b, :],
                              g_parts[:, :], start=True, stop=True)
                last.then_inc(gates_done, 1)

            def turn(bank_x, src, par, done):
                for j in range(TILES):
                    last = nc.tensor.transpose(bank_x[:, j * P:(j + 1) * P], tile(src, par, j), ident[:, :])
                last.then_inc(done, 1)

            def half(k, g0, q):
                r, t, h = k % RING, k // 2, k % 2
                if g0 >= 1 or k >= RING:
                    pe.wait_ge(e_used[r], 2 * g0 + k // RING + 2 * q)
                cols = slice(4 * h * P, (4 * h + 4) * P)
                hi, lo = tile(h2_hi, g0 % 2, t), tile(h2_lo, g0 % 2, t)
                mm(ring[r][:, :], hi, expert_w_hi[:, cols], start=True, stop=False)
                mm(ring[r][:, :], hi, expert_w_lo[:, cols], start=False, stop=False)
                mm(ring[r][:, :], lo, expert_w_hi[:, cols], start=False, stop=True).then_inc(e_ready[r], 1)

            def output_product(g2, q, b):
                if g2 == 0:
                    keep_clock(bank_a, 8)
                pe.wait_ge(y_ready, g2 + 1 + q)
                if g2 == 0:
                    pe.wait_ge(gab_ready, 1)
                    pe.wait_ge(outw_ready, 1)
                mm(bank_a[:, :], pick_bf[:, bass.ds(b, 1), :].rearrange("p b n -> p (b n)"),
                   gab_parts[:, :].unsqueeze(1).to_broadcast([3 * PART, TILES, P]),
                   start=True, stop=False)
                for j in range(TILES):
                    last = mm(bank_a[:, j * P:(j + 1) * P], tile(y_t, g2 % 2, j),
                              w_outg[:, bass.ds(b, 1), :].rearrange("p b n -> p (b n)"),
                              start=False, stop=(j == TILES - 1))
                last.then_inc(o_ready, 1)

            def turn_xn2(g1, q):
                pe.wait_ge(xn2_ready, g1 + 1 + q)
                if g1 >= 1:
                    pe.wait_ge(sub_ready, g1 + q)
                turn(bank_b, xn2, g1 % 2, x1t_ready)

            def mixed_bias(g, q):
                pe.wait_ge(wt_copied, g + 1 + q)
                mm(bank_v[:, :], w_parts_t[:, g % 2, :], expert_b_parts[:, :], start=True,
                   stop=True).then_inc(bias_ready, 1)

            def logits(g1, q):
                if g1 < groups - 1:
                    pe.wait_ge(h2_ready, g1 + 1 + q)
                else:
                    pe.wait_ge(h2_made, g1 + 1)
                    pe.wait_ge(x1_ready, g1 + 1)
                bank_l = logit_bank(g1)
                mm(bank_l[:, 0:TE], ones[0:1, 0:P].bitcast(F32), gate_b[:, :], start=True, stop=False)
                for j in range(TILES):
                    last = mm(bank_l[:, j * experts:(j + 1) * experts], tile(h2_t, g1 % 2, j),
                              gate_w[:, :], start=False, stop=(j == TILES - 1))
                last.then_inc(logit_ready, 1)

            def turn_parts(g0, gates, q):
                pe.wait_ge(wp_ready, g0 + 1 + q)
                pe.wait_ge(gate_done, gates + q)
                if gates == groups:
                    pe.wait_ge(wt_copied, g0)
                nc.tensor.transpose(bank_g[0:3 * TE, 0:P],
                                    w_parts[:, :, :].bitcast(F32).rearrange("p a b -> p (a b)"),
                                    ident[:, :]).then_inc(wt_ready, 1)

            def step(s, i):
                q = SLOTS * i
                g2, g1, g0, gt = s + 2, s + 1, s, s - 1
                bq = (SLOTS // per_batch) * i
                A, B, E, T = 0 <= g2 < groups, 0 <= g1 < groups, 0 <= g0 < groups, 0 <= gt < groups
                if s == -2:
                    gate_rows()
                if s == -3:
                    keep_clock(ring[0], 8)
                if s == 0:
                    pe.wait_ge(lo_ready, 1)
                    pe.wait_ge(gb_ready, 1)
                if A:
                    pe.wait_ge(h1_ready, g2 + 1 + q)
                    if g2 == 0:
                        pe.wait_ge(w_in_in, 16)
                        pe.wait_ge(v_bias_ready, 1)
                    if g0 >= 1:
                        pe.wait_ge(mix_ready, g0 + q)
                    mm(bank_v[:, :], b_v_parts[:, :], ones[:, :], start=True, stop=False)
                    mm(bank_v[:, :], w_in[:, 0:P], h1_t[:, g2 % 2, :], start=False,
                       stop=True).then_inc(v_ready, 1)
                    if g0 >= 1:
                        pe.wait_ge(wt_copied, g0 + q)
                    mm(bank_g[:, :], w_in[:, P:2 * P], h1_t[:, g2 % 2, :], start=True,
                       stop=True).then_inc(g_ready, 1)
                if g2 == 1:
                    keep_clock(bank_b, 10)
                if E:
                    pe.wait_ge(h2_split, g0 + 1 + q)
                    half(0, g0, q)
                    half(1, g0, q)
                    half(2, g0, q)
                if s == -1:
                    output_product(g2, 0, g2 // per_batch)
                if B:
                    turn_xn2(g1, q)
                if T:
                    if gt == 0:
                        pe.wait_ge(bias_parts_ready, 1)
                    pe.wait_ge(scan_done, g2 + 1 + q)
                    mixed_bias(gt, q)
                if A and s != -1:
                    output_product(g2, q, g2 // per_batch + bq)
                if E:
                    half(3, g0, q)
                if s == -1:
                    keep_clock(bank_v, 6)
                if B:
                    if g1 == 0:
                        pe.wait_ge(vectors_in, 16 * 5)
                        pe.wait_ge(late_in, 16 * 3)
                    logits(g1, q)
                if E:
                    half(4, g0, q)
                if 0 <= g2 + 1 < groups:
                    pe.wait_ge(xn1_ready, g2 + 2 + q)
                    if g2 >= 1:
                        pe.wait_ge(x1_ready, g2 + 1 + q)
                    turn(bank_b if g2 + 1 == 1 else bank_a, xn1, (g2 + 1) % 2, xt_ready)
                if s == -1:
                    keep_clock(bank_v, 3)
                if E:
                    turn_parts(g0, min(g2 + 1, groups), q)
                    half(5, g0, q)
                    half(6, g0, q)
                    half(7, g0, q)

            def ending():
                a, b, c = groups - 3, groups - 2, groups - 1
                pe.wait_ge(h2_split, b + 1)
                half(0, b, 0)
                half(1, b, 0)
                half(2, b, 0)
                turn_xn2(c, 0)
                pe.wait_ge(mix_ready, a + 1)
                mixed_bias(a, 0)
                half(3, b, 0)
                logits(c, 0)
                half(4, b, 0)
                turn_parts(b, groups, 0)
                half(5, b, 0)
                half(6, b, 0)
                half(7, b, 0)
                pe.wait_ge(h2_split, c + 1)
                half(0, c, 0)
                half(2, c, 0)
                pe.wait_ge(mix_ready, b + 1)
                mixed_bias(b, 0)
                half(1, c, 0)
                turn_parts(c, groups, 0)
                half(3, c, 0)
                half(4, c, 0)
                half(5, c, 0)
                half(6, c, 0)
                pe.wait_ge(mix_ready, c + 1)
                mixed_bias(c, 0)
                half(7, c, 0)

            steps(pe, step, -3, groups - 3)
            ending()


_INS = ["L0_attn_x", "L0_attn_W_in", "L0_attn_b_in", "L0_attn_A", "L0_attn_C", "L0_attn_W_out",
        "L0_attn_b_out", "L0_ffn_gate_w", "L0_ffn_gate_b", "L0_ffn_expert_w", "L0_ffn_expert_b",
        "L0_c", "L0_wmod"]
_OUTS = [((8, 1024, 128), "float32")]


def kernel(**inputs):
    import numpy as _np
    import concourse.bacc as _bacc
    from concourse import mybir as _mybir
    from concourse.bass_utils import run_bass_kernel_spmd as _run

    nc = _bacc.Bacc("TRN2", target_bir_lowering=False, num_devices=1)
    arrays, args = {}, []
    for name in _INS:
        a = _np.ascontiguousarray(inputs[name])
        arrays[f"in_{name}_dram"] = a
        args.append(nc.dram_tensor(f"in_{name}_dram", a.shape, _mybir.dt.from_np(a.dtype), kind="ExternalInput").ap())
    for i, (shape, dtype) in enumerate(_OUTS):
        dt = _mybir.dt.from_np(_np.dtype(dtype))
        args.append(nc.dram_tensor(f"out_{i}_dram", shape, dt, kind="ExternalOutput").ap())
    adaln_kernel(nc, *args)
    r = _run(nc, [arrays], core_ids=[0])
    return r.results[0]["out_0_dram"]
```
